# Optimizing a Trainium2 kernel written in Bass

```python
import numpy as np
import jax
import jax.numpy as jnp

def _softmax(x, axis=-1):
    return jax.nn.softmax(x, axis=axis)

def _gelu(x):
    return jax.nn.gelu(x, approximate=True)

def _silu(x):
    return jax.nn.silu(x)

def _sigmoid(x):
    return jax.nn.sigmoid(x)

def _layernorm(x, axis=-1, eps=1e-05):
    m = jnp.mean(x, axis=axis, keepdims=True)
    v = jnp.var(x, axis=axis, keepdims=True)
    return (x - m) / jnp.sqrt(v + eps)

def _scatter_add(tgt, idx, src, axis=0):
    return tgt.at[idx].add(src)

def _segment_sum(src, seg, n):
    return jax.ops.segment_sum(src, seg, n)
kernel_name = 'mk_adaln_ffn_d1_seqx_r8_6b32dc'

def setup_inputs(seed: int=0):
    np.random.seed(seed)
    _w = jnp.asarray

    def _rec_inputs():
        import jax
        import jax.numpy as jnp
        _rk = jax.random.key(seed)
        x = -0.000125 + 0.9999 * jax.random.normal(jax.random.fold_in(_rk, 1), (4, 256, 256), jnp.float32)
        _lenS = 256 - jax.random.randint(jax.random.fold_in(_rk, 7), (4,), 0, max(1, 256 // 4) + 1, jnp.int32)
        _lenS2 = 256 - jax.random.randint(jax.random.fold_in(_rk, 8), (4,), 0, max(1, 256 // 4) + 1, jnp.int32)
        itok_B_0_15 = jax.random.randint(jax.random.fold_in(_rk, 11), (4,), 0, 16, jnp.int32)
        return (x, itok_B_0_15)
    x, itok_B_0_15 = _rec_inputs()

    def _L0_cond_setup():
        import jax, jax.numpy as jnp
        import numpy as np
        key = jax.random.key(seed)
        k1, k2, k3, k4 = jax.random.split(key, 4)
        B, S, IN, OUT, E = (64, 32, 256, 256, 16)
        bound = 1.0 / np.sqrt(IN)
        x = jax.random.normal(k1, (B, S, IN), dtype=jnp.float32)
        idx = jax.random.randint(k2, (B,), 0, E, dtype=jnp.int64)
        W = jax.random.uniform(k3, (E, IN, OUT), dtype=jnp.float32, minval=-bound, maxval=bound)
        b = jnp.full((E, OUT), 0.1, dtype=jnp.float32)
        return {'x': x, 'id': idx, 'W': W, 'b': b}
    _L0_cond_all = _L0_cond_setup()
    _L0_cond_in = {k: v for k, v in _L0_cond_all.items() if k in ('W', 'b')}
    del _L0_cond_all

    def _L0_ffn_setup():
        import jax, jax.numpy as jnp
        import numpy as np
        D = 256
        F = 176
        E = 8
        TOPK = 2
        N_SHARED = 2
        ROUTE_SCALE = 1.0

        def _swiglu(x, w1, w2, w3):
            return jax.nn.silu(x @ w1) * (x @ w3) @ w2
        key = jax.random.key(seed)
        ks = jax.random.split(key, 8)
        s = 0.02
        x = jax.random.normal(ks[0], (2, 128, D), dtype=jnp.float32)
        gate_w = jax.random.normal(ks[1], (D, E), dtype=jnp.float32) * s
        Fs = F * N_SHARED
        sw1 = jax.random.normal(ks[2], (D, Fs), dtype=jnp.float32) * s
        sw2 = jax.random.normal(ks[3], (Fs, D), dtype=jnp.float32) * s
        sw3 = jax.random.normal(ks[4], (D, Fs), dtype=jnp.float32) * s
        rw1 = jax.random.normal(ks[5], (E, D, F), dtype=jnp.float32) * s
        rw2 = jax.random.normal(ks[6], (E, F, D), dtype=jnp.float32) * s
        rw3 = jax.random.normal(ks[7], (E, D, F), dtype=jnp.float32) * s
        return {'x': x, 'gate_w': gate_w, 'sw1': sw1, 'sw2': sw2, 'sw3': sw3, 'rw1': rw1, 'rw2': rw2, 'rw3': rw3}
    _L0_ffn_all = _L0_ffn_setup()
    _L0_ffn_in = {k: v for k, v in _L0_ffn_all.items() if k in ('gate_w', 'sw1', 'sw2', 'sw3', 'rw1', 'rw2', 'rw3')}
    del _L0_ffn_all
    return {'x': x, 'itok_B_0_15': itok_B_0_15, 'L0_cond_W': _L0_cond_in['W'], 'L0_cond_b': _L0_cond_in['b'], 'L0_ffn_gate_w': _L0_ffn_in['gate_w'], 'L0_ffn_sw1': _L0_ffn_in['sw1'], 'L0_ffn_sw2': _L0_ffn_in['sw2'], 'L0_ffn_sw3': _L0_ffn_in['sw3'], 'L0_ffn_rw1': _L0_ffn_in['rw1'], 'L0_ffn_rw2': _L0_ffn_in['rw2'], 'L0_ffn_rw3': _L0_ffn_in['rw3']}

def reference(x, itok_B_0_15, L0_cond_W, L0_cond_b, L0_ffn_gate_w, L0_ffn_sw1, L0_ffn_sw2, L0_ffn_sw3, L0_ffn_rw1, L0_ffn_rw2, L0_ffn_rw3):
    import jax
    import jax.numpy as jnp

    def _L0_cond_ref(x, id, W, b):
        import jax, jax.numpy as jnp
        import numpy as np
        Wg = W[id]
        bg = b[id]
        out = jnp.einsum('bsi,bio->bso', x, Wg) + bg[:, None, :]
        return out

    def _L0_ffn_ref(x, gate_w, sw1, sw2, sw3, rw1, rw2, rw3):
        import jax, jax.numpy as jnp
        import numpy as np
        D = 256
        F = 176
        E = 8
        TOPK = 2
        N_SHARED = 2
        ROUTE_SCALE = 1.0

        def _swiglu(x, w1, w2, w3):
            return jax.nn.silu(x @ w1) * (x @ w3) @ w2
        B, T, _ = x.shape
        xf = x.reshape(-1, D)
        N = xf.shape[0]
        y = _swiglu(xf, sw1, sw2, sw3)
        scores = jax.nn.softmax(xf @ gate_w, axis=-1)
        weights, indices = jax.lax.top_k(scores, TOPK)
        weights = weights * ROUTE_SCALE
        cw = jnp.zeros((N, E), dtype=xf.dtype).at[jnp.arange(N)[:, None], indices].add(weights)
        for e in range(E):
            h = _swiglu(xf, rw1[e], rw2[e], rw3[e])
            y = y + cw[:, e:e + 1] * h
        return y.reshape(B, T, D)
    x = x + _L0_ffn_ref(_L0_cond_ref(x, itok_B_0_15, L0_cond_W, L0_cond_b), L0_ffn_gate_w, L0_ffn_sw1, L0_ffn_sw2, L0_ffn_sw3, L0_ffn_rw1, L0_ffn_rw2, L0_ffn_rw3)
    return x

_drawn_inputs = setup_inputs


def setup_inputs(seed=0):
    import zlib

    import numpy as np

    out = dict(_drawn_inputs(seed))
    spreads = {'L0_cond_b': (0.10000000149011612, 0.6)}
    factors = {'L0_cond_W': 8.0,
     'L0_ffn_gate_w': 8.0,
     'L0_ffn_sw1': 8.0,
     'L0_ffn_sw2': 8.0,
     'L0_ffn_sw3': 8.0,
     'L0_ffn_rw1': 8.0,
     'L0_ffn_rw2': 8.0,
     'L0_ffn_rw3': 8.0}
    for name, (base, spread) in spreads.items():
        noise = np.random.default_rng([zlib.crc32(name.encode()), seed]).standard_normal(out[name].shape)
        drawn = base * np.exp(spread * noise) if base else spread * noise
        out[name] = jnp.asarray(drawn.astype(out[name].dtype))
    for name, factor in factors.items():
        out[name] = (out[name] * factor).astype(out[name].dtype)
    return out
```

```python
from contextlib import ExitStack

import concourse.bass as bass
from concourse import mybir

F32 = mybir.dt.float32
F32R = mybir.dt.float32r
BF16 = mybir.dt.bfloat16
ALU = mybir.AluOpType
ACT = mybir.ActivationFunctionType
AX = mybir.AxisListType

P = 128
NEG_HUGE = -3.0e38
WARM_MATMULS = 28


def adaln_moe_ffn(nc, x, ids, cond_w, cond_b, gate_w, sw1, sw2, sw3, rw1, rw2, rw3, out):
    B, S, D = x.shape
    E, _, F = rw1.shape
    FS = sw1.shape[1]
    KD = D // P
    TOK = B * S
    HALVES = 2
    HT = TOK // HALVES
    BH = B // HALVES
    JS = S // P
    NT = TOK // P
    M0 = FS % P
    NSH = -(-FS // P)
    NR = E * F // P
    NCH = NSH + NR
    assert KD == 2 and HT == 512 and M0 + E <= P and E * F % P == 0 and NSH == 3 and NR % 2 == 1

    dram_wT = nc.dram_tensor("route_weights_by_expert", [E * NT, P], F32, kind="Internal").ap()

    with ExitStack() as ctx:
        def sb(name, shape, dt=F32):
            return ctx.enter_context(nc.sbuf_tensor(name, shape, dt))

        def sem(name):
            return ctx.enter_context(nc.semaphore(name))

        x_sb = sb("x_sb", [P, B, JS, D])
        xT_hi = sb("xT_hi", [P, B, KD * S], F32R)
        xT_lo = sb("xT_lo", [P, B, KD * S], F32R)
        cw_hi = sb("cw_hi", [P, B, KD, D], F32R)
        cw_lo = sb("cw_lo", [P, B, KD, D], F32R)
        bias_rows = sb("bias_rows", [B, D])
        biasT = sb("biasT", [P, KD, B])
        hT_hi = sb("hT_hi", [P, KD, TOK], F32R)
        hT_lo = sb("hT_lo", [P, KD, TOK], F32R)
        w13_raw = sb("w13_raw", [P, 2 * KD, NCH * P])
        w2_raw = sb("w2_raw", [P, NCH, D])
        w13_hi = [sb(f"w13_hi{i}", [P, 2 * KD, P], F32R) for i in range(2)]
        w13_lo = [sb(f"w13_lo{i}", [P, 2 * KD, P], F32R) for i in range(2)]
        w2_hi = [sb(f"w2_hi{i}", [P, D], F32R) for i in range(2)]
        w2_lo = [sb(f"w2_lo{i}", [P, D], F32R) for i in range(2)]
        silu_a = [sb(f"silu_a{h}", [P, HT]) for h in range(HALVES)]
        gated = [sb(f"gated{h}", [P, HT]) for h in range(HALVES)]
        hidden = [sb(f"hidden{h}", [P, HT]) for h in range(HALVES)]
        g_hi = [[sb(f"g_hi{i}_{h}", [P, HT], F32R) for h in range(HALVES)] for i in range(3)]
        g_lo = [[sb(f"g_lo{i}_{h}", [P, HT], F32R) for h in range(HALVES)] for i in range(3)]
        route_bc = sb("route_bc", [P, NR, TOK])
        cw_raw = route_bc[:, 0:B * KD * D // TOK, :].rearrange("p r t -> p (r t)") \
            .rearrange("p (b k d) -> p b k d", b=B, k=KD)
        ident = sb("ident", [P, P])
        zeros = sb("zeros", [P, HT], BF16)
        logitT = sb("logitT", [E, TOK])
        first_rank = sb("first_rank", [P, NT, E])
        logit = sb("logit", [P, NT, E])
        top = [sb(f"top{i}", [P, NT]) for i in range(2)]
        hit = [sb(f"hit{i}", [P, NT, E]) for i in range(2)]
        hit_rank = [sb(f"hit_rank{i}", [P, NT, E]) for i in range(2)]
        best_rank = [sb(f"best_rank{i}", [P, NT]) for i in range(2)]
        chosen = [sb(f"chosen{i}", [P, NT, E]) for i in range(2)]
        others = sb("others", [P, NT, E])
        shifted = sb("shifted", [P, NT, E])
        expd = sb("expd", [P, NT, E])
        exp_sum = sb("exp_sum", [P, NT])
        exp_inv = sb("exp_inv", [P, NT])
        both = sb("both", [P, NT, E])
        picked = sb("picked", [P, NT, E])
        route = sb("route", [P, E, NT])
        routeT = sb("routeT", [E * NT, P])
        yT_sb = [[silu_a[h], gated[h]] for h in range(HALVES)]

        bank = [ctx.enter_context(nc.psum_tensor(f"bank{i}", [P, 512], F32)) for i in range(8)]
        up_a = [bank[0], bank[2]]
        up_b = [bank[1], bank[3]]
        y_acc = [[bank[4], bank[5]], [bank[6], bank[7]]]
        xT_ps = [bank[4], bank[5], bank[6], bank[7]]
        h_ps = [bank[0], bank[1], bank[2], bank[3]]
        bias_ps = bank[3]
        logit_ps = bank[6]
        routeT_ps = bank[7]
        yout_ps = [bank[0], bank[1], bank[2], bank[3]]

        x_in = [sem(f"x_in{b}") for b in range(B)]
        cw_in = [sem(f"cw_in{b}") for b in range(B)]
        bias_in = sem("bias_in")
        up0_in = sem("up0_in")
        down0_in = sem("down0_in")
        up12_in = sem("up12_in")
        down12_in = sem("down12_in")
        routed_in = sem("routed_in")
        routeT_out = sem("routeT_out")
        route_in = sem("route_in")
        zeros_ready = sem("zeros_ready")
        ident_ready = sem("ident_ready")
        rank_ready = sem("rank_ready")
        xT_ready = sem("xT_ready")
        xT_hi_ready = sem("xT_hi_ready")
        xT_lo_ready = sem("xT_lo_ready")
        cw_hi_ready = sem("cw_hi_ready")
        cw_lo_ready = sem("cw_lo_ready")
        bias_ps_ready = sem("bias_ps_ready")
        biasT_ready = sem("biasT_ready")
        h_ready = sem("h_ready")
        hT_hi_ready = sem("hT_hi_ready")
        hT_lo_ready = sem("hT_lo_ready")
        w13_hi_ready = sem("w13_hi_ready")
        w13_lo_ready = sem("w13_lo_ready")
        w2_hi_ready = sem("w2_hi_ready")
        w2_lo_ready = sem("w2_lo_ready")
        a_ready = [sem(f"a_ready{h}") for h in range(HALVES)]
        b_ready = [sem(f"b_ready{h}") for h in range(HALVES)]
        down_done = sem("down_done")
        silu_ready = [sem(f"silu_ready{h}") for h in range(HALVES)]
        gated_ready = [sem(f"gated_ready{h}") for h in range(HALVES)]
        weighed_ready = [sem(f"weighed_ready{h}") for h in range(HALVES)]
        g_hi_ready = [sem(f"g_hi_ready{h}") for h in range(HALVES)]
        g_lo_ready = [sem(f"g_lo_ready{h}") for h in range(HALVES)]
        logitT_ready = sem("logitT_ready")
        logit_ps_ready = sem("logit_ps_ready")
        logit_ready = sem("logit_ready")
        shifted_ready = sem("shifted_ready")
        expd_ready = sem("expd_ready")
        routing = sem("routing")
        route_ready = sem("route_ready")
        routeT_ps_ready = sem("routeT_ps_ready")
        routeT_ready = sem("routeT_ready")
        y_done = [sem(f"y_done{h}") for h in range(HALVES)]
        yT_copied = [[sem(f"yT_copied{h}_{d}") for d in range(KD)] for h in range(HALVES)]
        yout_ready = sem("yout_ready")
        out_ready = sem("out_ready")
        out_stored = sem("out_stored")

        x_tiled = x.rearrange("b (p j) d -> b p j d", j=JS)
        out_tiled = out.rearrange("b (p j) d -> b p (j d)", j=JS)
        cond_w_tiled = cond_w.rearrange("e (k p) o -> e p k o", p=P)

        def slot(c):
            return 2 if c == 0 else c % 2

        def units(c):
            return M0 if c == 0 else P

        block = ctx.enter_context(nc.Block())

        @block.sync
        def _(sp):
            for b in range(B):
                sp.dma_start(x_sb[:, b], x_tiled[b]).then_inc(x_in[b], 16)
                if b == 1:
                    for w, src in ((0, sw1), (1, sw3)):
                        sp.dma_start(w13_raw[:, KD * w:KD * w + KD, 0:M0],
                                     src[:, FS - M0:FS].rearrange("(k p) f -> p k f", p=P)).then_inc(up0_in, 16)
                    sp.dma_start(w13_raw[:, 0:KD, M0:M0 + E],
                                 gate_w.rearrange("(k p) e -> p k e", p=P)).then_inc(up0_in, 16)
            for w, src in ((0, sw1), (1, sw3)):
                sp.dma_start(w13_raw[:, KD * w:KD * w + KD, P:NSH * P],
                             src[:, 0:FS - M0].rearrange("(k p) f -> p k f", p=P)).then_inc(up12_in, 16)
            sp.dma_start(w2_raw[0:M0, 0, :], sw2[FS - M0:FS, :]).then_inc(down0_in, 16)
            sp.dma_start(w2_raw[:, 1:NSH, :],
                         sw2[0:FS - M0, :].rearrange("(c p) d -> p c d", p=P)).then_inc(down12_in, 16)
            for w, src in ((0, rw1), (1, rw3)):
                for k in range(KD):
                    sp.dma_start(w13_raw[:, KD * w + k, NSH * P:].rearrange("p (e f) -> p e f", e=E),
                                 src[:, k * P:k * P + P, :].rearrange("e p f -> p e f")).then_inc(routed_in, 16)
            sp.dma_start(w2_raw[:, NSH:, :],
                         rw2.rearrange("e f d -> (e f) d").rearrange("(c p) d -> p c d", p=P)).then_inc(routed_in, 16)

            sp.wait_ge(routeT_ready, 1)
            sp.dma_start(dram_wT, routeT[:, :]).then_inc(routeT_out, 16)
            sp.wait_ge(routeT_out, 16)
            for r in range(NR):
                unit = r * P
                while unit < (r + 1) * P:
                    e = unit // F
                    end = min((e + 1) * F, (r + 1) * P)
                    row = dram_wT[e * NT:(e + 1) * NT, :].rearrange("t c -> (t c)").unsqueeze(0)
                    sp.dma_start(route_bc[unit - r * P:end - r * P, r, :],
                                 row.to_broadcast([end - unit, TOK])).then_inc(route_in, 16)
                    unit = end

            for b in range(B):
                sp.wait_ge(out_ready, b + 1)
                sp.dma_start(out_tiled[b], x_sb[:, b].rearrange("p j d -> p (j d)")).then_inc(out_stored, 16)
            sp.wait_ge(out_stored, 16 * B)

        segments = sum(((r + 1) * P - 1) // F - r * P // F + 1 for r in range(NR))

        @block.gpsimd
        def _(pool):
            nc.gpsimd.memset(ident[:, :], 0.0).then_inc(ident_ready, 1)
            pool.wait_ge(ident_ready, 1)
            nc.gpsimd.affine_select(out=ident[:, :], in_=ident[:, :], compare_op=ALU.not_equal, fill=1.0,
                                    base=0, pattern=[[-1, P]], channel_multiplier=1).then_inc(ident_ready, 1)

            def lo_part(out_lo, raw, hi):
                return nc.gpsimd.tensor_tensor(out_lo, raw, hi.bitcast(F32), ALU.subtract)

            def cond_lo(b):
                pool.wait_ge(cw_hi_ready, b + 1)
                lo_part(cw_lo[:, b], cw_raw[:, b], cw_hi[:, b]).then_inc(cw_lo_ready, 1)

            def w13_lo_of(c, i, first=False):
                if not first:
                    pool.wait_ge(b_ready[-1], c - 1)
                pool.wait_ge(w13_hi_ready, c + 1)
                lo_part(w13_lo[i][:, :, :], w13_raw[:, :, bass.ds(c * P, P)], w13_hi[i][:, :, :]) \
                    .then_inc(w13_lo_ready, 1)

            def w2_lo_of(c, i, first=False):
                if not first:
                    pool.wait_ge(down_done, c - 1)
                pool.wait_ge(w2_hi_ready, c + 1)
                lo_part(w2_lo[i][:, :], w2_raw[:, c, :] if isinstance(c, int) else
                        w2_raw[:, bass.ds(c, 1), :].rearrange("p c d -> p (c d)"),
                        w2_hi[i][:, :]).then_inc(w2_lo_ready, 1)

            cond_lo(0)
            cond_lo(1)
            pool.wait_ge(w13_hi_ready, 1)
            lo_part(w13_lo[0][:, 0:KD, 0:M0 + E], w13_raw[:, 0:KD, 0:M0 + E], w13_hi[0][:, 0:KD, 0:M0 + E])
            lo_part(w13_lo[0][:, KD:, 0:M0], w13_raw[:, KD:, 0:M0], w13_hi[0][:, KD:, 0:M0]) \
                .then_inc(w13_lo_ready, 1)
            cond_lo(2)
            cond_lo(3)
            w13_lo_of(1, 1, first=True)
            pool.wait_ge(w2_hi_ready, 1)
            lo_part(w2_lo[0][0:M0, :], w2_raw[0:M0, 0, :], w2_hi[0][0:M0, :]).then_inc(w2_lo_ready, 1)
            w13_lo_of(2, 0)
            w2_lo_of(1, 1, first=True)
            w13_lo_of(3, 1)
            w2_lo_of(2, 0)
            with pool.Fori(0, NR - 2, 2) as r0:
                for j in range(2):
                    c = r0 + (NSH + j)
                    w13_lo_of(c + 1, (NSH + j + 1) % 2)
                    w2_lo_of(c, (NSH + j) % 2)
            w2_lo_of(NCH - 1, (NCH - 1) % 2)

        @block.scalar
        def _(act):
            expert = []
            for b in range(B):
                expert.append(nc.scalar.value_load(ids[0:1, b:b + 1], min_val=0, max_val=cond_w.shape[0] - 1))
                act.dma_start(cw_raw[:, b].unsqueeze(1), cond_w_tiled[bass.ds(expert[b], 1)].rearrange("e p k o -> p e k o")).then_inc(cw_in[b], 16)
            for b in range(B):
                act.dma_start(bias_rows[b:b + 1, :], cond_b[bass.ds(expert[b], 1), :]).then_inc(bias_in, 16)
            nc.scalar.preload_act_table(ACT.Silu)

            def xT_hi_of(b):
                act.wait_ge(xT_ready, b + 1)
                nc.scalar.copy(xT_hi[:, b, :], xT_ps[b][:, :]).then_inc(xT_hi_ready, 1)

            def hT_hi_of(b):
                act.wait_ge(h_ready, b + 1)
                if b == 0:
                    act.wait_ge(biasT_ready, 1)
                for m in range(KD):
                    nc.scalar.activation(hT_hi[:, m, b * S:(b + 1) * S], h_ps[b][:, m * S:(m + 1) * S], ACT.Identity,
                                         bias=biasT[:, m, b:b + 1]).then_inc(hT_hi_ready, 1)

            def w13_hi_of(c, i, first=False):
                if not first:
                    act.wait_ge(b_ready[-1], c - 1)
                nc.scalar.copy(w13_hi[i][:, :, :], w13_raw[:, :, bass.ds(c * P, P)]).then_inc(w13_hi_ready, 1)

            def w2_hi_of(c, i, first=False):
                if not first:
                    act.wait_ge(down_done, c - 1)
                nc.scalar.copy(w2_hi[i][:, :], w2_raw[:, c, :] if isinstance(c, int) else
                               w2_raw[:, bass.ds(c, 1), :].rearrange("p c d -> p (c d)")).then_inc(w2_hi_ready, 1)

            def silu_of(c, h, n=P, first=False):
                act.wait_ge(a_ready[h], c + 1)
                if not first:
                    act.wait_ge(gated_ready[h], c)
                nc.scalar.activation(silu_a[h][0:n, :], up_a[h][0:n, :], ACT.Silu).then_inc(silu_ready[h], 1)

            def g_hi_of(c, h, i, n=P, shared=False, reused=True):
                if shared:
                    act.wait_ge(gated_ready[h], c + 1)
                else:
                    act.wait_ge(weighed_ready[h], c + (1 - NSH))
                if reused:
                    act.wait_ge(down_done, c - 1)
                nc.scalar.copy(g_hi[i][h][0:n, :], hidden[h][0:n, :]).then_inc(g_hi_ready[h], 1)

            xT_hi_of(0)
            xT_hi_of(1)
            act.wait_ge(up0_in, 48)
            nc.scalar.copy(w13_hi[0][:, 0:KD, 0:M0 + E], w13_raw[:, 0:KD, 0:M0 + E])
            nc.scalar.copy(w13_hi[0][:, KD:, 0:M0], w13_raw[:, KD:, 0:M0]).then_inc(w13_hi_ready, 1)
            hT_hi_of(0)
            xT_hi_of(2)
            hT_hi_of(1)
            xT_hi_of(3)
            act.wait_ge(up12_in, 32)
            w13_hi_of(1, 1, first=True)
            silu_of(0, 0, n=M0, first=True)
            hT_hi_of(2)
            hT_hi_of(3)
            g_hi_of(0, 0, slot(0), n=M0, shared=True, reused=False)
            silu_of(0, 1, n=M0, first=True)
            act.wait_ge(down0_in, 16)
            nc.scalar.copy(w2_hi[0][0:M0, :], w2_raw[0:M0, 0, :]).then_inc(w2_hi_ready, 1)
            g_hi_of(0, 1, slot(0), n=M0, shared=True, reused=False)
            w13_hi_of(2, 0)
            silu_of(1, 0)
            act.wait_ge(shifted_ready, 1)
            nc.scalar.activation(expd[:, :, :], shifted[:, :, :], ACT.Exp).then_inc(expd_ready, 1)
            g_hi_of(1, 0, slot(1), shared=True, reused=False)
            act.wait_ge(down12_in, 16)
            w2_hi_of(1, 1, first=True)
            silu_of(1, 1)
            g_hi_of(1, 1, slot(1), shared=True, reused=False)
            act.wait_ge(routed_in, 16 * (2 * KD + 1))
            w13_hi_of(3, 1)
            silu_of(2, 0)
            act.wait_ge(routeT_ps_ready, 1)
            nc.scalar.copy(routeT[:, :], routeT_ps[0:E * NT, 0:P]).then_inc(routeT_ready, 1)
            g_hi_of(2, 0, slot(2), shared=True, reused=False)
            silu_of(2, 1)
            g_hi_of(2, 1, slot(2), shared=True, reused=False)
            w2_hi_of(2, 0)

            def routed_chunk(c, i, last=False):
                if not last:
                    w13_hi_of(c + 1, 1 - i)
                for h in range(HALVES):
                    silu_of(c, h)
                for h in range(HALVES):
                    g_hi_of(c, h, i)
                w2_hi_of(c, i)

            with act.Fori(0, NR - 2, 2) as r0:
                for j in range(2):
                    routed_chunk(r0 + (NSH + j), (NSH + j) % 2)
            routed_chunk(NCH - 1, (NCH - 1) % 2, last=True)

            for h in range(HALVES):
                act.wait_ge(y_done[h], 1)
                nc.scalar.copy(yT_sb[h][0][:, :], y_acc[h][0][:, :]).then_inc(yT_copied[h][0], 1)

        @block.vector
        def _(dve):
            nc.vector.memset(zeros[:, :], 0.0).then_inc(zeros_ready, 1)
            for e in range(E):
                last = nc.vector.memset(first_rank[:, :, e:e + 1], float(E - e))
            last.then_inc(rank_ready, 1)

            def lo_part(out_lo, value, hi):
                return nc.vector.tensor_tensor(out_lo, value, hi.bitcast(F32), ALU.subtract)

            def cond_hi(b):
                dve.wait_ge(cw_in[b], 16)
                nc.vector.tensor_copy(cw_hi[:, b], cw_raw[:, b]).then_inc(cw_hi_ready, 1)

            def xT_lo_of(b):
                dve.wait_ge(xT_hi_ready, b + 1)
                lo_part(xT_lo[:, b, :], xT_ps[b][:, :], xT_hi[:, b, :]).then_inc(xT_lo_ready, 1)

            def hT_lo_of(b):
                dve.wait_ge(hT_hi_ready, KD * (b + 1))
                for m in range(KD):
                    cols = slice(b * S, (b + 1) * S)
                    nc.vector.scalar_tensor_tensor(
                        out=hT_lo[:, m, cols], in0=h_ps[b][:, m * S:(m + 1) * S], scalar=biasT[:, m, b:b + 1],
                        in1=hT_hi[:, m, cols].bitcast(F32), op0=ALU.add, op1=ALU.subtract).then_inc(hT_lo_ready, 1)

            def gate(c, h, n=P, shared=False, first=False):
                dve.wait_ge(silu_ready[h], c + 1)
                dve.wait_ge(b_ready[h], c + 1)
                if shared and not first:
                    dve.wait_ge(g_hi_ready[h], c)
                    dve.wait_ge(g_lo_ready[h], c)
                dst = hidden[h] if shared else gated[h]
                nc.vector.tensor_tensor(dst[0:n, :], silu_a[h][0:n, :], up_b[h][0:n, :], ALU.mult) \
                    .then_inc(gated_ready[h], 1)

            def weigh(r, h):
                dve.wait_ge(gated_ready[h], r + (NSH + 1))
                dve.wait_ge(g_hi_ready[h], r + NSH)
                dve.wait_ge(g_lo_ready[h], r + NSH)
                bc = route_bc[:, bass.ds(r, 1), h * HT:(h + 1) * HT].rearrange("p r t -> p (r t)")
                nc.vector.tensor_tensor(hidden[h][:, :], gated[h][:, :], bc, ALU.mult).then_inc(weighed_ready[h], 1)

            def g_lo_of(c, h, i, n=P):
                dve.wait_ge(g_hi_ready[h], c + 1)
                lo_part(g_lo[i][h][0:n, :], hidden[h][0:n, :], g_hi[i][h][0:n, :]).then_inc(g_lo_ready[h], 1)

            def logitT_of(h):
                dve.wait_ge(a_ready[h], 1)
                nc.vector.tensor_copy(logitT[:, h * HT:(h + 1) * HT], up_a[h][M0:M0 + E, :]).then_inc(logitT_ready, 1)

            cond_hi(0)
            cond_hi(1)
            xT_lo_of(0)
            xT_lo_of(1)
            dve.wait_ge(bias_ps_ready, 1)
            nc.vector.tensor_copy(biasT[:, :, :], bias_ps[:, 0:KD * B].rearrange("p (m b) -> p m b", b=B)) \
                .then_inc(biasT_ready, 1)
            dve.wait_ge(biasT_ready, 1)
            cond_hi(2)
            hT_lo_of(0)
            xT_lo_of(2)
            cond_hi(3)
            hT_lo_of(1)
            xT_lo_of(3)
            logitT_of(0)
            gate(0, 0, n=M0, shared=True, first=True)
            hT_lo_of(2)
            hT_lo_of(3)
            g_lo_of(0, 0, slot(0), n=M0)
            logitT_of(1)
            gate(0, 1, n=M0, shared=True, first=True)
            g_lo_of(0, 1, slot(0), n=M0)
            gate(1, 0, shared=True)

            chain = [0]

            def link(instruction):
                chain[0] += 1
                instruction.then_inc(routing, 1)
                dve.wait_ge(routing, chain[0])

            def over_experts(t):
                return t[:, :].unsqueeze(2).to_broadcast([P, NT, E])

            dve.wait_ge(logit_ps_ready, 1)
            link(nc.vector.tensor_copy(logit[:, :, :], logit_ps[:, 0:NT * E].rearrange("p (t e) -> p t e", e=E)))
            source = logit
            for i in range(2):
                link(nc.vector.tensor_reduce(top[i][:, :], source[:, :, :], AX.X, ALU.max))
                if i == 0:
                    nc.vector.tensor_tensor(shifted[:, :, :], logit[:, :, :], over_experts(top[0]), ALU.subtract) \
                        .then_inc(shifted_ready, 1)
                    dve.wait_ge(rank_ready, 1)
                link(nc.vector.tensor_tensor(hit[i][:, :, :], source[:, :, :], over_experts(top[i]), ALU.is_equal))
                link(nc.vector.tensor_tensor(hit_rank[i][:, :, :], hit[i][:, :, :], first_rank[:, :, :], ALU.mult))
                link(nc.vector.tensor_reduce(best_rank[i][:, :], hit_rank[i][:, :, :], AX.X, ALU.max))
                link(nc.vector.tensor_tensor(chosen[i][:, :, :], hit_rank[i][:, :, :], over_experts(best_rank[i]),
                                             ALU.is_equal))
                if i == 0:
                    link(nc.vector.scalar_tensor_tensor(out=others[:, :, :], in0=chosen[0][:, :, :], scalar=NEG_HUGE,
                                                        in1=logit[:, :, :], op0=ALU.mult, op1=ALU.add))
                    source = others
            link(nc.vector.tensor_tensor(both[:, :, :], chosen[0][:, :, :], chosen[1][:, :, :], ALU.add))
            dve.wait_ge(expd_ready, 1)
            nc.vector.tensor_tensor(picked[:, :, :], both[:, :, :], expd[:, :, :], ALU.mult)
            link(nc.vector.tensor_reduce(exp_sum[:, :], expd[:, :, :], AX.X, ALU.add))
            link(nc.vector.reciprocal(exp_inv[:, :], exp_sum[:, :]))
            nc.vector.tensor_tensor(route[:, :, :].rearrange("p e t -> p t e"), picked[:, :, :], over_experts(exp_inv),
                                    ALU.mult).then_inc(route_ready, 1)

            g_lo_of(1, 0, slot(1))
            gate(1, 1, shared=True)
            g_lo_of(1, 1, slot(1))
            for h in range(HALVES):
                gate(2, h, shared=True)
                g_lo_of(2, h, slot(2))

            def routed_chunk(r, i):
                for h in range(HALVES):
                    gate(r + NSH, h)
                    weigh(r, h)
                for h in range(HALVES):
                    g_lo_of(r + NSH, h, i)

            dve.wait_ge(route_in, 16 * segments)
            with dve.Fori(0, NR - 2, 2) as r0:
                for j in range(2):
                    routed_chunk(r0 + j, (NSH + j) % 2)
            routed_chunk(NR - 1, (NCH - 1) % 2)

            for h in range(HALVES):
                dve.wait_ge(y_done[h], 1)
                nc.vector.tensor_copy(yT_sb[h][1][:, :], y_acc[h][1][:, :]).then_inc(yT_copied[h][1], 1)
            for b in range(B):
                dve.wait_ge(yout_ready, b + 1)
                x_row = x_sb[:, b].rearrange("p j d -> p (j d)")
                nc.vector.tensor_tensor(x_row, yout_ps[b][:, :], x_row, ALU.add).then_inc(out_ready, 1)

        @block.tensor
        def _(pe):
            pe.wait_ge(zeros_ready, 1)
            for _ in range(WARM_MATMULS):
                nc.tensor.matmul(bank[2][:, :], zeros[:, 0:P], zeros[:, :], start=True, stop=True)

            def turn_x(b):
                pe.wait_ge(x_in[b], 16)
                for k in range(KD):
                    for j in range(JS):
                        last = nc.tensor.transpose(xT_ps[b][:, k * S + j * P:k * S + (j + 1) * P],
                                                   x_sb[:, b, j, k * P:(k + 1) * P], ident[:, :])
                last.then_inc(xT_ready, 1)

            def three_passes(dst, n, pairs, start, stop):
                total = len(pairs) * 3
                done = 0
                for w_hi, w_lo, v_hi, v_lo in pairs:
                    for w, v in ((w_hi, v_hi), (w_lo, v_hi), (w_hi, v_lo)):
                        last = nc.tensor.matmul(dst, w, v, start=start and done == 0, stop=stop and done == total - 1)
                        done += 1
                return last

            def condition(b):
                pe.wait_ge(xT_hi_ready, b + 1)
                pe.wait_ge(xT_lo_ready, b + 1)
                pe.wait_ge(cw_hi_ready, b + 1)
                pe.wait_ge(cw_lo_ready, b + 1)
                for m in range(KD):
                    cols = slice(m * P, (m + 1) * P)
                    last = three_passes(h_ps[b][:, m * S:(m + 1) * S], P,
                                        [(cw_hi[:, b, k, cols], cw_lo[:, b, k, cols],
                                          xT_hi[:, b, k * S:(k + 1) * S], xT_lo[:, b, k * S:(k + 1) * S])
                                         for k in range(KD)], True, True)
                last.then_inc(h_ready, 1)

            def up(c, h, i, rows=(P, P), first=False):
                pe.wait_ge(w13_hi_ready, c + 1)
                pe.wait_ge(w13_lo_ready, c + 1)
                if not first:
                    pe.wait_ge(gated_ready[h], c)
                toks = slice(h * HT, (h + 1) * HT)
                for w, (dst, ready) in enumerate(((up_a[h], a_ready[h]), (up_b[h], b_ready[h]))):
                    n = rows[w]
                    last = three_passes(dst[0:n, :], n,
                                        [(w13_hi[i][:, KD * w + k, 0:n], w13_lo[i][:, KD * w + k, 0:n],
                                          hT_hi[:, k, toks], hT_lo[:, k, toks]) for k in range(KD)], True, True)
                    last.then_inc(ready, 1)

            def down(c, h, wi, gi, n=P, start=False, stop=False):
                pe.wait_ge(w2_hi_ready, c + 1)
                pe.wait_ge(w2_lo_ready, c + 1)
                pe.wait_ge(g_hi_ready[h], c + 1)
                pe.wait_ge(g_lo_ready[h], c + 1)
                for d in range(KD):
                    cols = slice(d * P, (d + 1) * P)
                    last = three_passes(y_acc[h][d][:, :], P,
                                        [(w2_hi[wi][0:n, cols], w2_lo[wi][0:n, cols],
                                          g_hi[gi][h][0:n, :], g_lo[gi][h][0:n, :])], start, stop)
                if stop:
                    last.then_inc(y_done[h], 1)
                elif h == HALVES - 1:
                    last.then_inc(down_done, 1)

            pe.wait_ge(ident_ready, 2)
            turn_x(0)
            turn_x(1)
            pe.wait_ge(bias_in, 16 * B)
            for m in range(KD):
                last = nc.tensor.transpose(bias_ps[:, m * B:(m + 1) * B], bias_rows[:, m * P:(m + 1) * P],
                                           ident[0:B, 0:B])
            last.then_inc(bias_ps_ready, 1)
            condition(0)
            turn_x(2)
            condition(1)
            turn_x(3)
            pe.wait_ge(hT_hi_ready, KD * 2)
            pe.wait_ge(hT_lo_ready, KD * 2)
            up(0, 0, 0, rows=(M0 + E, M0), first=True)
            condition(2)
            pe.wait_ge(biasT_ready, 1)
            condition(3)
            pe.wait_ge(hT_hi_ready, KD * B)
            pe.wait_ge(hT_lo_ready, KD * B)
            up(0, 1, 0, rows=(M0 + E, M0), first=True)
            up(1, 0, 1)
            pe.wait_ge(logitT_ready, HALVES)
            for t in range(NT):
                last = nc.tensor.transpose(logit_ps[:, t * E:(t + 1) * E], logitT[:, t * P:(t + 1) * P],
                                           ident[0:E, 0:E])
            last.then_inc(logit_ps_ready, 1)
            up(1, 1, 1)
            up(2, 0, 0)
            pe.wait_ge(route_ready, 1)
            nc.tensor.transpose(routeT_ps[0:E * NT, 0:P], route[:, :, :].rearrange("p e t -> p (e t)"), ident[:, :]) \
                .then_inc(routeT_ps_ready, 1)
            up(2, 1, 0)
            down(0, 0, 0, slot(0), n=M0, start=True)
            pe.wait_ge(routeT_ready, 1)
            down(0, 1, 0, slot(0), n=M0, start=True)
            for h in range(HALVES):
                down(1, h, 1, slot(1))

            def routed_chunk(c, i):
                for h in range(HALVES):
                    up(c, h, i)
                for h in range(HALVES):
                    down(c - 1, h, 1 - i, 1 - i)

            with pe.Fori(0, NR - 2, 2) as r0:
                for j in range(2):
                    routed_chunk(r0 + (NSH + j), (NSH + j) % 2)
            routed_chunk(NCH - 1, (NCH - 1) % 2)
            for h in range(HALVES):
                down(NCH - 1, h, (NCH - 1) % 2, (NCH - 1) % 2, stop=True)

            for b in range(B):
                h = b // BH
                if b % BH == 0:
                    for d in range(KD):
                        pe.wait_ge(yT_copied[h][d], 1)
                for j in range(JS):
                    for d in range(KD):
                        at = (b % BH) * S + j * P
                        last = nc.tensor.transpose(yout_ps[b][:, j * D + d * P:j * D + (d + 1) * P],
                                                   yT_sb[h][d][:, at:at + P], ident[:, :])
                last.then_inc(yout_ready, 1)


_INS = ['x', 'itok_B_0_15', 'L0_cond_W', 'L0_cond_b', 'L0_ffn_gate_w', 'L0_ffn_sw1', 'L0_ffn_sw2', 'L0_ffn_sw3',
        'L0_ffn_rw1', 'L0_ffn_rw2', 'L0_ffn_rw3']


def kernel(**inputs):
    import numpy as _np
    import concourse.bacc as _bacc
    from concourse import mybir as _mybir
    from concourse.bass_utils import run_bass_kernel_spmd as _run

    nc = _bacc.Bacc("TRN2", target_bir_lowering=False, num_devices=1)
    arrays, args = {}, []
    for name in _INS:
        a = _np.ascontiguousarray(inputs[name])
        if name == 'itok_B_0_15':
            a = a.reshape(1, -1)
        arrays[f"in_{name}_dram"] = a
        args.append(nc.dram_tensor(f"in_{name}_dram", a.shape, _mybir.dt.from_np(a.dtype), kind="ExternalInput").ap())
    x = arrays["in_x_dram"]
    out = nc.dram_tensor("out_dram", x.shape, _mybir.dt.from_np(x.dtype), kind="ExternalOutput").ap()
    adaln_moe_ffn(nc, *args, out)
    r = _run(nc, [arrays], core_ids=[0])
    return r.results[0]["out_dram"]
```

```python
from contextlib import ExitStack

import concourse.bass as bass
from concourse import mybir

F32 = mybir.dt.float32
F32R = mybir.dt.float32r
BF16 = mybir.dt.bfloat16
ALU = mybir.AluOpType
ACT = mybir.ActivationFunctionType
AX = mybir.AxisListType

P = 128
NEG_HUGE = -3.0e38
WARM_BEFORE_X = 6
WARM_BEFORE_CONDITION = 4


def adaln_moe_ffn(nc, x, ids, cond_w, cond_b, gate_w, sw1, sw2, sw3, rw1, rw2, rw3, out):
    B, S, D = x.shape
    E, _, F = rw1.shape
    FS = sw1.shape[1]
    KD = D // P
    TOK = B * S
    HALVES = 2
    HT = TOK // HALVES
    BH = B // HALVES
    JS = S // P
    NT = TOK // P
    M0 = FS % P
    NSH = -(-FS // P)
    NR = E * F // P
    NCH = NSH + NR
    assert KD == 2 and HT == 512 and M0 + E <= P and E * F % P == 0 and NSH == 3 and NR % 2 == 1

    dram_wT = nc.dram_tensor("route_weights_by_expert", [E * NT, P], F32, kind="Internal").ap()

    with ExitStack() as ctx:
        def sb(name, shape, dt=F32):
            return ctx.enter_context(nc.sbuf_tensor(name, shape, dt))

        def sem(name):
            return ctx.enter_context(nc.semaphore(name))

        x_sb = sb("x_sb", [P, B, JS, D])
        xT_hi = sb("xT_hi", [P, B, KD * S], F32R)
        xT_lo = sb("xT_lo", [P, B, KD * S], F32R)
        cw_hi = sb("cw_hi", [P, B, KD, D], F32R)
        cw_lo = sb("cw_lo", [P, B, KD, D], F32R)
        NE = cond_b.shape[0]
        bias_rows = sb("bias_rows", [NE, D])
        ids_bc = sb("ids_bc", [NE, B], ids.dtype)
        expert_no = sb("expert_no", [NE, 1], mybir.dt.int32)
        one_hot = sb("one_hot", [NE, B])
        biasT = sb("biasT", [P, KD, B])
        hT_hi = sb("hT_hi", [P, KD, TOK], F32R)
        hT_lo = sb("hT_lo", [P, KD, TOK], F32R)
        w13_raw = sb("w13_raw", [P, 2 * KD, NCH * P])
        w2_raw = sb("w2_raw", [P, NCH, D])
        w13_hi = [sb(f"w13_hi{i}", [P, 2 * KD, P], F32R) for i in range(2)]
        w13_lo = [sb(f"w13_lo{i}", [P, 2 * KD, P], F32R) for i in range(2)]
        w2_hi = [sb(f"w2_hi{i}", [P, D], F32R) for i in range(2)]
        w2_lo = [sb(f"w2_lo{i}", [P, D], F32R) for i in range(2)]
        silu_a = [sb(f"silu_a{h}", [P, HT]) for h in range(HALVES)]
        gated = [sb(f"gated{h}", [P, HT]) for h in range(HALVES)]
        hidden = [sb(f"hidden{h}", [P, HT]) for h in range(HALVES)]
        g_hi = [[sb(f"g_hi{i}_{h}", [P, HT], F32R) for h in range(HALVES)] for i in range(3)]
        g_lo = [[sb(f"g_lo{i}_{h}", [P, HT], F32R) for h in range(HALVES)] for i in range(3)]
        route_bc = sb("route_bc", [P, NR, TOK])
        cw_raw = route_bc[:, 0:B * KD * D // TOK, :].rearrange("p r t -> p (r t)") \
            .rearrange("p (b k d) -> p b k d", b=B, k=KD)
        ident = sb("ident", [P, P])
        zeros = sb("zeros", [P, HT], BF16)
        logitT = sb("logitT", [E, TOK])
        first_rank = sb("first_rank", [P, NT, E])
        logit = sb("logit", [P, NT, E])
        top = [sb(f"top{i}", [P, NT]) for i in range(2)]
        hit = [sb(f"hit{i}", [P, NT, E]) for i in range(2)]
        hit_rank = [sb(f"hit_rank{i}", [P, NT, E]) for i in range(2)]
        best_rank = [sb(f"best_rank{i}", [P, NT]) for i in range(2)]
        chosen = [sb(f"chosen{i}", [P, NT, E]) for i in range(2)]
        others = sb("others", [P, NT, E])
        shifted = sb("shifted", [P, NT, E])
        expd = sb("expd", [P, NT, E])
        exp_sum = sb("exp_sum", [P, NT])
        exp_inv = sb("exp_inv", [P, NT])
        both = sb("both", [P, NT, E])
        picked = sb("picked", [P, NT, E])
        route = sb("route", [P, E, NT])
        routeT = sb("routeT", [E * NT, P])
        yT_sb = [[silu_a[h], gated[h]] for h in range(HALVES)]

        bank = [ctx.enter_context(nc.psum_tensor(f"bank{i}", [P, 512], F32)) for i in range(8)]
        up_a = [bank[0], bank[2]]
        up_b = [bank[1], bank[3]]
        y_acc = [[bank[4], bank[5]], [bank[6], bank[7]]]
        xT_ps = [bank[4], bank[5], bank[6], bank[7]]
        h_ps = [bank[0], bank[1], bank[2], bank[3]]
        bias_ps = bank[3]
        logit_ps = bank[6]
        routeT_ps = bank[7]
        yout_ps = [bank[0], bank[1], bank[2], bank[3]]

        x_in = [sem(f"x_in{b}") for b in range(B)]
        cw_in = [sem(f"cw_in{b}") for b in range(B)]
        bias_in = sem("bias_in")
        up0_in = sem("up0_in")
        down0_in = sem("down0_in")
        up12_in = sem("up12_in")
        down12_in = sem("down12_in")
        routed_up_in = [sem(f"routed_up_in{g}") for g in range(2)]
        routed_down_in = sem("routed_down_in")
        routeT_out = sem("routeT_out")
        route_in = [sem(f"route_in{g}") for g in range(2)]
        zeros_ready = sem("zeros_ready")
        ident_ready = sem("ident_ready")
        rank_ready = sem("rank_ready")
        expert_no_ready = sem("expert_no_ready")
        one_hot_ready = sem("one_hot_ready")
        xT_ready = sem("xT_ready")
        xT_hi_ready = sem("xT_hi_ready")
        xT_lo_ready = sem("xT_lo_ready")
        cw_hi_ready = sem("cw_hi_ready")
        cw_lo_ready = sem("cw_lo_ready")
        bias_ps_ready = sem("bias_ps_ready")
        biasT_ready = sem("biasT_ready")
        h_ready = sem("h_ready")
        hT_hi_ready = sem("hT_hi_ready")
        hT_lo_ready = sem("hT_lo_ready")
        w13_hi_ready = sem("w13_hi_ready")
        w13_lo_ready = sem("w13_lo_ready")
        w2_hi_ready = sem("w2_hi_ready")
        w2_lo_ready = sem("w2_lo_ready")
        a_ready = [sem(f"a_ready{h}") for h in range(HALVES)]
        b_ready = [sem(f"b_ready{h}") for h in range(HALVES)]
        down_done = sem("down_done")
        silu_ready = [sem(f"silu_ready{h}") for h in range(HALVES)]
        gated_ready = [sem(f"gated_ready{h}") for h in range(HALVES)]
        weighed_ready = [sem(f"weighed_ready{h}") for h in range(HALVES)]
        g_hi_ready = [sem(f"g_hi_ready{h}") for h in range(HALVES)]
        g_lo_ready = [sem(f"g_lo_ready{h}") for h in range(HALVES)]
        logitT_ready = sem("logitT_ready")
        logit_ps_ready = sem("logit_ps_ready")
        logit_ready = sem("logit_ready")
        shifted_ready = sem("shifted_ready")
        expd_ready = sem("expd_ready")
        routing = sem("routing")
        route_ready = sem("route_ready")
        routeT_ps_ready = sem("routeT_ps_ready")
        routeT_ready = sem("routeT_ready")
        y_done = [sem(f"y_done{h}") for h in range(HALVES)]
        yT_copied = [[sem(f"yT_copied{h}_{d}") for d in range(KD)] for h in range(HALVES)]
        yout_ready = sem("yout_ready")
        out_ready = sem("out_ready")
        out_stored = sem("out_stored")

        x_tiled = x.rearrange("b (p j) d -> b p j d", j=JS)
        out_tiled = out.rearrange("b (p j) d -> b p (j d)", j=JS)
        cond_w_tiled = cond_w.rearrange("e (k p) o -> e p k o", p=P)

        def slot(c):
            return 2 if c == 0 else c % 2

        def units(c):
            return M0 if c == 0 else P

        PEELED = 2
        LOOP = (PEELED, NR - 2, 2)
        assert (NSH + PEELED + 1) * P <= NSH * P + E // 2 * F and (NR - 1 - PEELED) % 2 == 0

        block = ctx.enter_context(nc.Block())

        @block.sync
        def _(sp):
            def condition_in(b, expert):
                sp.dma_start(cw_raw[:, b].unsqueeze(1),
                             cond_w_tiled[bass.ds(expert, 1)].rearrange("e p k o -> p e k o")).then_inc(cw_in[b], 16)

            expert = [nc.sync.value_load(ids[0:1, b:b + 1], min_val=0, max_val=NE - 1) for b in range(BH)]
            for b in range(BH):
                condition_in(b, expert[b])
            for w, src in ((0, sw1), (1, sw3)):
                sp.dma_start(w13_raw[:, KD * w:KD * w + KD, 0:M0],
                             src[:, FS - M0:FS].rearrange("(k p) f -> p k f", p=P)).then_inc(up0_in, 16)
            sp.dma_start(w13_raw[:, 0:KD, M0:M0 + E],
                         gate_w.rearrange("(k p) e -> p k e", p=P)).then_inc(up0_in, 16)
            expert = [nc.sync.value_load(ids[0:1, b:b + 1], min_val=0, max_val=NE - 1) for b in range(BH, B)]
            for b in range(BH, B):
                condition_in(b, expert[b - BH])
            for w, src in ((0, sw1), (1, sw3)):
                sp.dma_start(w13_raw[:, KD * w:KD * w + KD, P:NSH * P],
                             src[:, 0:FS - M0].rearrange("(k p) f -> p k f", p=P)).then_inc(up12_in, 16)
            sp.dma_start(w2_raw[0:M0, 0, :], sw2[FS - M0:FS, :]).then_inc(down0_in, 16)
            sp.dma_start(w2_raw[:, 1:NSH, :],
                         sw2[0:FS - M0, :].rearrange("(c p) d -> p c d", p=P)).then_inc(down12_in, 16)
            for g in range(2):
                for w, src in ((0, rw1), (1, rw3)):
                    for k in range(KD):
                        units_g = slice(NSH * P + g * E // 2 * F, NSH * P + (g + 1) * E // 2 * F)
                        sp.dma_start(w13_raw[:, KD * w + k, units_g].rearrange("p (e f) -> p e f", e=E // 2),
                                     src[g * E // 2:(g + 1) * E // 2, k * P:k * P + P, :]
                                     .rearrange("e p f -> p e f")).then_inc(routed_up_in[g], 16)
                if g == 0:
                    sp.dma_start(w2_raw[:, NSH:, :], rw2.rearrange("e f d -> (e f) d")
                                 .rearrange("(c p) d -> p c d", p=P)).then_inc(routed_down_in, 16)

            sp.wait_ge(routeT_ready, 1)
            sp.dma_start(dram_wT, routeT[:, :]).then_inc(routeT_out, 16)
            sp.wait_ge(routeT_out, 16)
            for r in range(NR):
                unit = r * P
                while unit < (r + 1) * P:
                    e = unit // F
                    end = min((e + 1) * F, (r + 1) * P)
                    row = dram_wT[e * NT:(e + 1) * NT, :].rearrange("t c -> (t c)").unsqueeze(0)
                    sp.dma_start(route_bc[unit - r * P:end - r * P, r, :],
                                 row.to_broadcast([end - unit, TOK])).then_inc(route_in[r >= PEELED], 16)
                    unit = end

            for b in range(B):
                sp.wait_ge(out_ready, b + 1)
                sp.dma_start(out_tiled[b], x_sb[:, b].rearrange("p j d -> p (j d)")).then_inc(out_stored, 16)
            sp.wait_ge(out_stored, 16 * B)

        def segments(chunks):
            return sum(((r + 1) * P - 1) // F - r * P // F + 1 for r in chunks)

        @block.gpsimd
        def _(pool):
            nc.gpsimd.memset(ident[:, :], 0.0).then_inc(ident_ready, 1)
            pool.wait_ge(ident_ready, 1)
            nc.gpsimd.affine_select(out=ident[:, :], in_=ident[:, :], compare_op=ALU.not_equal, fill=1.0,
                                    base=0, pattern=[[-1, P]], channel_multiplier=1).then_inc(ident_ready, 1)
            nc.gpsimd.iota(expert_no[:, :], pattern=[[0, 1]], base=0, channel_multiplier=1).then_inc(expert_no_ready, 1)

            def lo_part(out_lo, raw, hi):
                return nc.gpsimd.tensor_tensor(out_lo, raw, hi.bitcast(F32), ALU.subtract)

            def cond_lo(b):
                pool.wait_ge(cw_hi_ready, b + 1)
                lo_part(cw_lo[:, b], cw_raw[:, b], cw_hi[:, b]).then_inc(cw_lo_ready, 1)

            def w13_lo_of(c, i, first=False):
                if not first:
                    pool.wait_ge(b_ready[-1], c - 1)
                pool.wait_ge(w13_hi_ready, c + 1)
                lo_part(w13_lo[i][:, :, :], w13_raw[:, :, bass.ds(c * P, P)], w13_hi[i][:, :, :]) \
                    .then_inc(w13_lo_ready, 1)

            def w2_lo_of(c, i, first=False):
                if not first:
                    pool.wait_ge(down_done, c - 1)
                pool.wait_ge(w2_hi_ready, c + 1)
                lo_part(w2_lo[i][:, :], w2_raw[:, c, :] if isinstance(c, int) else
                        w2_raw[:, bass.ds(c, 1), :].rearrange("p c d -> p (c d)"),
                        w2_hi[i][:, :]).then_inc(w2_lo_ready, 1)

            cond_lo(0)
            cond_lo(1)
            pool.wait_ge(w13_hi_ready, 1)
            lo_part(w13_lo[0][:, 0:KD, 0:M0 + E], w13_raw[:, 0:KD, 0:M0 + E], w13_hi[0][:, 0:KD, 0:M0 + E])
            lo_part(w13_lo[0][:, KD:, 0:M0], w13_raw[:, KD:, 0:M0], w13_hi[0][:, KD:, 0:M0]) \
                .then_inc(w13_lo_ready, 1)
            cond_lo(2)
            cond_lo(3)
            w13_lo_of(1, 1, first=True)
            pool.wait_ge(w2_hi_ready, 1)
            lo_part(w2_lo[0][0:M0, :], w2_raw[0:M0, 0, :], w2_hi[0][0:M0, :]).then_inc(w2_lo_ready, 1)
            w13_lo_of(2, 0)
            w2_lo_of(1, 1, first=True)
            w2_lo_of(2, 0)
            w13_lo_of(NSH, NSH % 2)
            for c in range(NSH, NSH + PEELED):
                w2_lo_of(c, c % 2)
                w13_lo_of(c + 1, (c + 1) % 2)
            with pool.Fori(*LOOP) as r0:
                for j in range(2):
                    c = r0 + (NSH + j)
                    w2_lo_of(c, (NSH + j) % 2)
                    w13_lo_of(c + 1, (NSH + j + 1) % 2)
            w2_lo_of(NCH - 1, (NCH - 1) % 2)

        @block.scalar
        def _(act):
            act.dma_start(x_sb[:, 0], x_tiled[0]).then_inc(x_in[0], 16)
            act.dma_start(x_sb[:, 1], x_tiled[1]).then_inc(x_in[1], 16)
            act.dma_start(ids_bc[:, :], ids.to_broadcast([NE, B])).then_inc(bias_in, 16)
            act.dma_start(bias_rows[:, :], cond_b).then_inc(bias_in, 16)
            act.dma_start(x_sb[:, 2], x_tiled[2]).then_inc(x_in[2], 16)
            act.dma_start(x_sb[:, 3], x_tiled[3]).then_inc(x_in[3], 16)
            nc.scalar.preload_act_table(ACT.Silu)

            def xT_hi_of(b):
                act.wait_ge(xT_ready, b + 1)
                nc.scalar.copy(xT_hi[:, b, :], xT_ps[b][:, :]).then_inc(xT_hi_ready, 1)

            def hT_hi_of(b):
                act.wait_ge(h_ready, b + 1)
                if b == 0:
                    act.wait_ge(biasT_ready, 1)
                for m in range(KD):
                    nc.scalar.activation(hT_hi[:, m, b * S:(b + 1) * S], h_ps[b][:, m * S:(m + 1) * S], ACT.Identity,
                                         bias=biasT[:, m, b:b + 1]).then_inc(hT_hi_ready, 1)

            def w13_hi_of(c, i, first=False):
                if not first:
                    act.wait_ge(b_ready[-1], c - 1)
                nc.scalar.copy(w13_hi[i][:, :, :], w13_raw[:, :, bass.ds(c * P, P)]).then_inc(w13_hi_ready, 1)

            def w2_hi_of(c, i, first=False):
                if not first:
                    act.wait_ge(down_done, c - 1)
                nc.scalar.copy(w2_hi[i][:, :], w2_raw[:, c, :] if isinstance(c, int) else
                               w2_raw[:, bass.ds(c, 1), :].rearrange("p c d -> p (c d)")).then_inc(w2_hi_ready, 1)

            def silu_of(c, h, n=P, first=False):
                act.wait_ge(a_ready[h], c + 1)
                if not first:
                    act.wait_ge(gated_ready[h], c)
                nc.scalar.activation(silu_a[h][0:n, :], up_a[h][0:n, :], ACT.Silu).then_inc(silu_ready[h], 1)

            def g_hi_of(c, h, i, n=P, shared=False, reused=True):
                if shared:
                    act.wait_ge(gated_ready[h], c + 1)
                else:
                    act.wait_ge(weighed_ready[h], c + (1 - NSH))
                if reused:
                    act.wait_ge(down_done, c - 1)
                nc.scalar.copy(g_hi[i][h][0:n, :], hidden[h][0:n, :]).then_inc(g_hi_ready[h], 1)

            xT_hi_of(0)
            xT_hi_of(1)
            act.wait_ge(up0_in, 48)
            nc.scalar.copy(w13_hi[0][:, 0:KD, 0:M0 + E], w13_raw[:, 0:KD, 0:M0 + E])
            nc.scalar.copy(w13_hi[0][:, KD:, 0:M0], w13_raw[:, KD:, 0:M0]).then_inc(w13_hi_ready, 1)
            hT_hi_of(0)
            xT_hi_of(2)
            hT_hi_of(1)
            xT_hi_of(3)
            act.wait_ge(up12_in, 32)
            w13_hi_of(1, 1, first=True)
            silu_of(0, 0, n=M0, first=True)
            hT_hi_of(2)
            hT_hi_of(3)
            g_hi_of(0, 0, slot(0), n=M0, shared=True, reused=False)
            silu_of(0, 1, n=M0, first=True)
            act.wait_ge(down0_in, 16)
            nc.scalar.copy(w2_hi[0][0:M0, :], w2_raw[0:M0, 0, :]).then_inc(w2_hi_ready, 1)
            g_hi_of(0, 1, slot(0), n=M0, shared=True, reused=False)
            w13_hi_of(2, 0)
            silu_of(1, 0)
            act.wait_ge(shifted_ready, 1)
            nc.scalar.activation(expd[:, :, :], shifted[:, :, :], ACT.Exp).then_inc(expd_ready, 1)
            g_hi_of(1, 0, slot(1), shared=True, reused=False)
            act.wait_ge(down12_in, 16)
            w2_hi_of(1, 1, first=True)
            silu_of(1, 1)
            g_hi_of(1, 1, slot(1), shared=True, reused=False)
            act.wait_ge(routed_up_in[0], 16 * 2 * KD)
            w13_hi_of(3, 1)
            silu_of(2, 0)
            act.wait_ge(routeT_ps_ready, 1)
            nc.scalar.copy(routeT[:, :], routeT_ps[0:E * NT, 0:P]).then_inc(routeT_ready, 1)
            g_hi_of(2, 0, slot(2), shared=True, reused=False)
            silu_of(2, 1)
            g_hi_of(2, 1, slot(2), shared=True, reused=False)
            w2_hi_of(2, 0)

            def routed_chunk(c, i, last=False):
                w2_hi_of(c, i)
                if not last:
                    w13_hi_of(c + 1, 1 - i)
                for h in range(HALVES):
                    silu_of(c, h)
                for h in range(HALVES):
                    g_hi_of(c, h, i)

            act.wait_ge(routed_down_in, 16)
            for c in range(NSH, NSH + PEELED):
                routed_chunk(c, c % 2)
            act.wait_ge(routed_up_in[1], 16 * 2 * KD)
            with act.Fori(*LOOP) as r0:
                for j in range(2):
                    routed_chunk(r0 + (NSH + j), (NSH + j) % 2)
            routed_chunk(NCH - 1, (NCH - 1) % 2, last=True)

            for h in range(HALVES):
                act.wait_ge(y_done[h], 1)
                nc.scalar.copy(yT_sb[h][0][:, :], y_acc[h][0][:, :]).then_inc(yT_copied[h][0], 1)

        @block.vector
        def _(dve):
            nc.vector.memset(zeros[:, :], 0.0).then_inc(zeros_ready, 1)
            for e in range(E):
                last = nc.vector.memset(first_rank[:, :, e:e + 1], float(E - e))
            last.then_inc(rank_ready, 1)

            def lo_part(out_lo, value, hi):
                return nc.vector.tensor_tensor(out_lo, value, hi.bitcast(F32), ALU.subtract)

            def cond_hi(b):
                dve.wait_ge(cw_in[b], 16)
                nc.vector.tensor_copy(cw_hi[:, b], cw_raw[:, b]).then_inc(cw_hi_ready, 1)

            def xT_lo_of(b):
                dve.wait_ge(xT_hi_ready, b + 1)
                lo_part(xT_lo[:, b, :], xT_ps[b][:, :], xT_hi[:, b, :]).then_inc(xT_lo_ready, 1)

            def hT_lo_of(b):
                dve.wait_ge(hT_hi_ready, KD * (b + 1))
                for m in range(KD):
                    cols = slice(b * S, (b + 1) * S)
                    nc.vector.scalar_tensor_tensor(
                        out=hT_lo[:, m, cols], in0=h_ps[b][:, m * S:(m + 1) * S], scalar=biasT[:, m, b:b + 1],
                        in1=hT_hi[:, m, cols].bitcast(F32), op0=ALU.add, op1=ALU.subtract).then_inc(hT_lo_ready, 1)

            def gate(c, h, n=P, shared=False, first=False):
                dve.wait_ge(silu_ready[h], c + 1)
                dve.wait_ge(b_ready[h], c + 1)
                if shared and not first:
                    dve.wait_ge(g_hi_ready[h], c)
                    dve.wait_ge(g_lo_ready[h], c)
                dst = hidden[h] if shared else gated[h]
                nc.vector.tensor_tensor(dst[0:n, :], silu_a[h][0:n, :], up_b[h][0:n, :], ALU.mult) \
                    .then_inc(gated_ready[h], 1)

            def weigh(r, h):
                dve.wait_ge(gated_ready[h], r + (NSH + 1))
                dve.wait_ge(g_hi_ready[h], r + NSH)
                dve.wait_ge(g_lo_ready[h], r + NSH)
                bc = route_bc[:, bass.ds(r, 1), h * HT:(h + 1) * HT].rearrange("p r t -> p (r t)")
                nc.vector.tensor_tensor(hidden[h][:, :], gated[h][:, :], bc, ALU.mult).then_inc(weighed_ready[h], 1)

            def g_lo_of(c, h, i, n=P):
                dve.wait_ge(g_hi_ready[h], c + 1)
                lo_part(g_lo[i][h][0:n, :], hidden[h][0:n, :], g_hi[i][h][0:n, :]).then_inc(g_lo_ready[h], 1)

            def logitT_of(h):
                dve.wait_ge(a_ready[h], 1)
                nc.vector.tensor_copy(logitT[:, h * HT:(h + 1) * HT], up_a[h][M0:M0 + E, :]).then_inc(logitT_ready, 1)

            dve.wait_ge(bias_in, 32)
            dve.wait_ge(expert_no_ready, 1)
            nc.vector.tensor_scalar(one_hot[:, :], ids_bc[:, :], expert_no[:, 0:1], None, ALU.is_equal) \
                .then_inc(one_hot_ready, 1)
            xT_lo_of(0)
            cond_hi(0)
            xT_lo_of(1)
            cond_hi(1)
            dve.wait_ge(bias_ps_ready, 1)
            nc.vector.tensor_copy(biasT[:, :, :], bias_ps[:, 0:KD * B].rearrange("p (m b) -> p m b", b=B)) \
                .then_inc(biasT_ready, 1)
            dve.wait_ge(biasT_ready, 1)
            cond_hi(2)
            hT_lo_of(0)
            xT_lo_of(2)
            cond_hi(3)
            hT_lo_of(1)
            xT_lo_of(3)
            logitT_of(0)
            gate(0, 0, n=M0, shared=True, first=True)
            hT_lo_of(2)
            hT_lo_of(3)
            g_lo_of(0, 0, slot(0), n=M0)
            logitT_of(1)
            gate(0, 1, n=M0, shared=True, first=True)
            g_lo_of(0, 1, slot(0), n=M0)
            gate(1, 0, shared=True)

            chain = [0]

            def link(instruction):
                chain[0] += 1
                instruction.then_inc(routing, 1)
                dve.wait_ge(routing, chain[0])

            def over_experts(t):
                return t[:, :].unsqueeze(2).to_broadcast([P, NT, E])

            dve.wait_ge(logit_ps_ready, 1)
            link(nc.vector.tensor_copy(logit[:, :, :], logit_ps[:, 0:NT * E].rearrange("p (t e) -> p t e", e=E)))
            source = logit
            for i in range(2):
                link(nc.vector.tensor_reduce(top[i][:, :], source[:, :, :], AX.X, ALU.max))
                if i == 0:
                    nc.vector.tensor_tensor(shifted[:, :, :], logit[:, :, :], over_experts(top[0]), ALU.subtract) \
                        .then_inc(shifted_ready, 1)
                    dve.wait_ge(rank_ready, 1)
                link(nc.vector.tensor_tensor(hit[i][:, :, :], source[:, :, :], over_experts(top[i]), ALU.is_equal))
                link(nc.vector.tensor_tensor(hit_rank[i][:, :, :], hit[i][:, :, :], first_rank[:, :, :], ALU.mult))
                link(nc.vector.tensor_reduce(best_rank[i][:, :], hit_rank[i][:, :, :], AX.X, ALU.max))
                link(nc.vector.tensor_tensor(chosen[i][:, :, :], hit_rank[i][:, :, :], over_experts(best_rank[i]),
                                             ALU.is_equal))
                if i == 0:
                    link(nc.vector.scalar_tensor_tensor(out=others[:, :, :], in0=chosen[0][:, :, :], scalar=NEG_HUGE,
                                                        in1=logit[:, :, :], op0=ALU.mult, op1=ALU.add))
                    source = others
            link(nc.vector.tensor_tensor(both[:, :, :], chosen[0][:, :, :], chosen[1][:, :, :], ALU.add))
            dve.wait_ge(expd_ready, 1)
            nc.vector.tensor_tensor(picked[:, :, :], both[:, :, :], expd[:, :, :], ALU.mult)
            link(nc.vector.tensor_reduce(exp_sum[:, :], expd[:, :, :], AX.X, ALU.add))
            link(nc.vector.reciprocal(exp_inv[:, :], exp_sum[:, :]))
            nc.vector.tensor_tensor(route[:, :, :].rearrange("p e t -> p t e"), picked[:, :, :], over_experts(exp_inv),
                                    ALU.mult).then_inc(route_ready, 1)

            g_lo_of(1, 0, slot(1))
            gate(1, 1, shared=True)
            g_lo_of(1, 1, slot(1))
            for h in range(HALVES):
                gate(2, h, shared=True)
                g_lo_of(2, h, slot(2))

            def routed_chunk(r, i):
                for h in range(HALVES):
                    gate(r + NSH, h)
                    weigh(r, h)
                for h in range(HALVES):
                    g_lo_of(r + NSH, h, i)

            dve.wait_ge(route_in[0], 16 * segments(range(PEELED)))
            for r in range(PEELED):
                routed_chunk(r, (NSH + r) % 2)
            dve.wait_ge(route_in[1], 16 * segments(range(PEELED, NR)))
            with dve.Fori(*LOOP) as r0:
                for j in range(2):
                    routed_chunk(r0 + j, (NSH + j) % 2)
            routed_chunk(NR - 1, (NCH - 1) % 2)

            for b in range(B):
                h = b // BH
                if b % BH == 0:
                    dve.wait_ge(y_done[h], KD)
                    for i in range(BH):
                        cols = slice(i * S, (i + 1) * S)
                        nc.vector.tensor_copy(yT_sb[h][1][:, cols], y_acc[h][1][:, cols]).then_inc(yT_copied[h][1], 1)
                dve.wait_ge(yout_ready, b + 1)
                x_row = x_sb[:, b].rearrange("p j d -> p (j d)")
                nc.vector.tensor_tensor(x_row, yout_ps[b][:, :], x_row, ALU.add).then_inc(out_ready, 1)

        @block.tensor
        def _(pe):
            pe.wait_ge(zeros_ready, 1)
            def keep_warm(times):
                for _ in range(times):
                    nc.tensor.matmul(bank[2][:, :], zeros[:, 0:P], zeros[:, :], start=True, stop=True)

            keep_warm(WARM_BEFORE_X)

            def turn_x(b):
                pe.wait_ge(x_in[b], 16)
                for k in range(KD):
                    for j in range(JS):
                        last = nc.tensor.transpose(xT_ps[b][:, k * S + j * P:k * S + (j + 1) * P],
                                                   x_sb[:, b, j, k * P:(k + 1) * P], ident[:, :])
                last.then_inc(xT_ready, 1)

            def three_passes(dst, n, pairs, start, stop):
                total = len(pairs) * 3
                done = 0
                for w_hi, w_lo, v_hi, v_lo in pairs:
                    for w, v in ((w_hi, v_hi), (w_lo, v_hi), (w_hi, v_lo)):
                        last = nc.tensor.matmul(dst, w, v, start=start and done == 0, stop=stop and done == total - 1)
                        done += 1
                return last

            def condition(b):
                pe.wait_ge(xT_hi_ready, b + 1)
                pe.wait_ge(xT_lo_ready, b + 1)
                pe.wait_ge(cw_hi_ready, b + 1)
                pe.wait_ge(cw_lo_ready, b + 1)
                for m in range(KD):
                    cols = slice(m * P, (m + 1) * P)
                    last = three_passes(h_ps[b][:, m * S:(m + 1) * S], P,
                                        [(cw_hi[:, b, k, cols], cw_lo[:, b, k, cols],
                                          xT_hi[:, b, k * S:(k + 1) * S], xT_lo[:, b, k * S:(k + 1) * S])
                                         for k in range(KD)], True, True)
                last.then_inc(h_ready, 1)

            def up(c, h, i, rows=(P, P), first=False):
                pe.wait_ge(w13_hi_ready, c + 1)
                pe.wait_ge(w13_lo_ready, c + 1)
                if not first:
                    pe.wait_ge(gated_ready[h], c)
                toks = slice(h * HT, (h + 1) * HT)
                for w, (dst, ready) in enumerate(((up_a[h], a_ready[h]), (up_b[h], b_ready[h]))):
                    n = rows[w]
                    last = three_passes(dst[0:n, :], n,
                                        [(w13_hi[i][:, KD * w + k, 0:n], w13_lo[i][:, KD * w + k, 0:n],
                                          hT_hi[:, k, toks], hT_lo[:, k, toks]) for k in range(KD)], True, True)
                    last.then_inc(ready, 1)

            def down(c, h, wi, gi, n=P, start=False, stop=False):
                pe.wait_ge(w2_hi_ready, c + 1)
                pe.wait_ge(w2_lo_ready, c + 1)
                pe.wait_ge(g_hi_ready[h], c + 1)
                pe.wait_ge(g_lo_ready[h], c + 1)
                for d in range(KD):
                    cols = slice(d * P, (d + 1) * P)
                    last = three_passes(y_acc[h][d][:, :], P,
                                        [(w2_hi[wi][0:n, cols], w2_lo[wi][0:n, cols],
                                          g_hi[gi][h][0:n, :], g_lo[gi][h][0:n, :])], start, stop)
                    if stop:
                        last.then_inc(y_done[h], 1)
                if not stop and h == HALVES - 1:
                    last.then_inc(down_done, 1)

            pe.wait_ge(ident_ready, 2)
            turn_x(0)
            turn_x(1)
            pe.wait_ge(one_hot_ready, 1)
            for m in range(KD):
                last = nc.tensor.matmul(bias_ps[:, m * B:(m + 1) * B], bias_rows[:, m * P:(m + 1) * P], one_hot[:, :],
                                        start=True, stop=True)
            last.then_inc(bias_ps_ready, 1)
            keep_warm(WARM_BEFORE_CONDITION)
            condition(0)
            turn_x(2)
            condition(1)
            turn_x(3)
            pe.wait_ge(hT_hi_ready, KD * 2)
            pe.wait_ge(hT_lo_ready, KD * 2)
            up(0, 0, 0, rows=(M0 + E, M0), first=True)
            condition(2)
            pe.wait_ge(biasT_ready, 1)
            condition(3)
            pe.wait_ge(hT_hi_ready, KD * B)
            pe.wait_ge(hT_lo_ready, KD * B)
            up(0, 1, 0, rows=(M0 + E, M0), first=True)
            up(1, 0, 1)
            pe.wait_ge(logitT_ready, HALVES)
            for t in range(NT):
                last = nc.tensor.transpose(logit_ps[:, t * E:(t + 1) * E], logitT[:, t * P:(t + 1) * P],
                                           ident[0:E, 0:E])
            last.then_inc(logit_ps_ready, 1)
            up(1, 1, 1)
            up(2, 0, 0)
            pe.wait_ge(route_ready, 1)
            nc.tensor.transpose(routeT_ps[0:E * NT, 0:P], route[:, :, :].rearrange("p e t -> p (e t)"), ident[:, :]) \
                .then_inc(routeT_ps_ready, 1)
            up(2, 1, 0)
            down(0, 0, 0, slot(0), n=M0, start=True)
            pe.wait_ge(routeT_ready, 1)
            down(0, 1, 0, slot(0), n=M0, start=True)
            for h in range(HALVES):
                down(1, h, 1, slot(1))

            def routed_chunk(c, i):
                for h in range(HALVES):
                    up(c, h, i)
                for h in range(HALVES):
                    down(c - 1, h, 1 - i, 1 - i)

            for c in range(NSH, NSH + PEELED):
                routed_chunk(c, c % 2)
            with pe.Fori(*LOOP) as r0:
                for j in range(2):
                    routed_chunk(r0 + (NSH + j), (NSH + j) % 2)
            i = (NCH - 1) % 2
            for h in range(HALVES):
                up(NCH - 1, h, i)
            for h in range(HALVES):
                down(NCH - 2, h, 1 - i, 1 - i)
                down(NCH - 1, h, i, i, stop=True)

            for b in range(B):
                h = b // BH
                pe.wait_ge(yT_copied[h][0], 1)
                pe.wait_ge(yT_copied[h][1], b % BH + 1)
                for j in range(JS):
                    for d in range(KD):
                        at = (b % BH) * S + j * P
                        last = nc.tensor.transpose(yout_ps[b][:, j * D + d * P:j * D + (d + 1) * P],
                                                   yT_sb[h][d][:, at:at + P], ident[:, :])
                last.then_inc(yout_ready, 1)


_INS = ['x', 'itok_B_0_15', 'L0_cond_W', 'L0_cond_b', 'L0_ffn_gate_w', 'L0_ffn_sw1', 'L0_ffn_sw2', 'L0_ffn_sw3',
        'L0_ffn_rw1', 'L0_ffn_rw2', 'L0_ffn_rw3']


def kernel(**inputs):
    import numpy as _np
    import concourse.bacc as _bacc
    from concourse import mybir as _mybir
    from concourse.bass_utils import run_bass_kernel_spmd as _run

    nc = _bacc.Bacc("TRN2", target_bir_lowering=False, num_devices=1)
    arrays, args = {}, []
    for name in _INS:
        a = _np.ascontiguousarray(inputs[name])
        if name == 'itok_B_0_15':
            a = a.reshape(1, -1)
        arrays[f"in_{name}_dram"] = a
        args.append(nc.dram_tensor(f"in_{name}_dram", a.shape, _mybir.dt.from_np(a.dtype), kind="ExternalInput").ap())
    x = arrays["in_x_dram"]
    out = nc.dram_tensor("out_dram", x.shape, _mybir.dt.from_np(x.dtype), kind="ExternalOutput").ap()
    adaln_moe_ffn(nc, *args, out)
    r = _run(nc, [arrays], core_ids=[0])
    return r.results[0]["out_dram"]
```

```python
from contextlib import ExitStack

import concourse.bass as bass
from concourse import mybir

F32 = mybir.dt.float32
F32R = mybir.dt.float32r
BF16 = mybir.dt.bfloat16
ALU = mybir.AluOpType
ACT = mybir.ActivationFunctionType
AX = mybir.AxisListType

P = 128
NEG_HUGE = -3.0e38
WARM_BEFORE_X = 13
WARM_BEFORE_CONDITION = 3


def adaln_moe_ffn(nc, x, ids, cond_w, cond_b, gate_w, sw1, sw2, sw3, rw1, rw2, rw3, out):
    B, S, D = x.shape
    E, _, F = rw1.shape
    FS = sw1.shape[1]
    KD = D // P
    TOK = B * S
    HALVES = 2
    HT = TOK // HALVES
    BH = B // HALVES
    JS = S // P
    NT = TOK // P
    M0 = FS % P
    NSH = -(-FS // P)
    NR = E * F // P
    NCH = NSH + NR
    assert KD == 2 and HT == 512 and M0 + E <= P and E * F % P == 0 and NSH == 3 and NR % 2 == 1

    dram_wT = nc.dram_tensor("route_weights_by_expert", [E * NT, P], F32, kind="Internal").ap()

    with ExitStack() as ctx:
        def sb(name, shape, dt=F32):
            return ctx.enter_context(nc.sbuf_tensor(name, shape, dt))

        def sem(name):
            return ctx.enter_context(nc.semaphore(name))

        x_sb = sb("x_sb", [P, B, JS, D])
        xT_f32 = sb("xT_f32", [P, BH, KD * S])
        xT_hi = sb("xT_hi", [P, BH, KD * S], F32R)
        xT_lo = sb("xT_lo", [P, BH, KD * S], F32R)
        cw_hi = sb("cw_hi", [P, BH, KD, D], F32R)
        cw_lo = sb("cw_lo", [P, BH, KD, D], F32R)
        NE = cond_b.shape[0]
        bias_rows = sb("bias_rows", [NE, D])
        ids_bc = sb("ids_bc", [NE, B], ids.dtype)
        expert_no = sb("expert_no", [NE, 1], mybir.dt.int32)
        one_hot = sb("one_hot", [NE, B])
        biasT = sb("biasT", [P, KD, B])
        hT_hi = sb("hT_hi", [P, KD, TOK], F32R)
        hT_lo = sb("hT_lo", [P, KD, TOK], F32R)
        w13_raw = sb("w13_raw", [P, 2 * KD, NCH * P])
        w2_raw = sb("w2_raw", [P, NCH, D])
        w13_hi = [sb(f"w13_hi{i}", [P, 2 * KD, P], F32R) for i in range(2)]
        w13_lo = [sb(f"w13_lo{i}", [P, 2 * KD, P], F32R) for i in range(2)]
        w2_hi = [sb(f"w2_hi{i}", [P, D], F32R) for i in range(2)]
        w2_lo = [sb(f"w2_lo{i}", [P, D], F32R) for i in range(2)]
        silu_a = [sb(f"silu_a{h}", [P, HT]) for h in range(HALVES)]
        gated = [sb(f"gated{h}", [P, HT]) for h in range(HALVES)]
        hidden = [sb(f"hidden{h}", [P, HT]) for h in range(HALVES)]
        g_hi = [[sb(f"g_hi{i}_{h}", [P, HT], F32R) for h in range(HALVES)] for i in range(3)]
        g_lo = [[sb(f"g_lo{i}_{h}", [P, HT], F32R) for h in range(HALVES)] for i in range(3)]
        route_bc = sb("route_bc", [P, NR, TOK])
        cw_raw = route_bc[:, 0:B * KD * D // TOK, :].rearrange("p r t -> p (r t)") \
            .rearrange("p (b k d) -> p b k d", b=B, k=KD)
        ident = sb("ident", [P, P])
        logitT = sb("logitT", [E, TOK])
        first_rank = sb("first_rank", [P, NT, E])
        logit = sb("logit", [P, NT, E])
        top = [sb(f"top{i}", [P, NT]) for i in range(2)]
        hit = [sb(f"hit{i}", [P, NT, E]) for i in range(2)]
        hit_rank = [sb(f"hit_rank{i}", [P, NT, E]) for i in range(2)]
        best_rank = [sb(f"best_rank{i}", [P, NT]) for i in range(2)]
        chosen = [sb(f"chosen{i}", [P, NT, E]) for i in range(2)]
        others = sb("others", [P, NT, E])
        shifted = sb("shifted", [P, NT, E])
        expd = sb("expd", [P, NT, E])
        exp_sum = sb("exp_sum", [P, NT])
        exp_inv = sb("exp_inv", [P, NT])
        both = sb("both", [P, NT, E])
        picked = sb("picked", [P, NT, E])
        route = sb("route", [P, E, NT])
        routeT = sb("routeT", [E * NT, P])

        bank = [ctx.enter_context(nc.psum_tensor(f"bank{i}", [P, 512], F32)) for i in range(8)]
        up_a = [bank[0], bank[2]]
        up_b = [bank[1], bank[3]]
        y_acc = [bank[4], bank[5], bank[6], bank[7]]
        xT_ps = [bank[4], bank[5], bank[6], bank[7]]
        h_ps = [[bank[0][:, 0:S], bank[1][:, 0:S]], [bank[2][:, 0:S], bank[3][:, 0:S]],
                [bank[4][:, 0:S], bank[4][:, S:2 * S]], [bank[5][:, 0:S], bank[5][:, S:2 * S]]]
        bias_ps = bank[7]
        logit_ps = bank[6]
        routeT_ps = bank[7]

        x_in = [sem(f"x_in{b}") for b in range(B)]
        cw_in = [sem(f"cw_in{b}") for b in range(B)]
        ids_in = sem("ids_in")
        bias_in = sem("bias_in")
        up0_in = sem("up0_in")
        down0_in = sem("down0_in")
        up12_in = sem("up12_in")
        down12_in = sem("down12_in")
        routed_up_in = [sem(f"routed_up_in{g}") for g in range(2)]
        routed_down_in = sem("routed_down_in")
        routeT_out = sem("routeT_out")
        route_in = [sem(f"route_in{g}") for g in range(2)]
        ident_ready = sem("ident_ready")
        rank_ready = sem("rank_ready")
        expert_no_ready = sem("expert_no_ready")
        one_hot_ready = sem("one_hot_ready")
        xT_ready = sem("xT_ready")
        xT_f32_ready = [sem(f"xT_f32_ready{b}") for b in range(BH)]
        xT_hi_ready = sem("xT_hi_ready")
        xT_lo_ready = sem("xT_lo_ready")
        cw_hi_ready = sem("cw_hi_ready")
        cw_lo_ready = sem("cw_lo_ready")
        bias_ps_ready = sem("bias_ps_ready")
        biasT_ready = sem("biasT_ready")
        h_ready = sem("h_ready")
        hT_hi_ready = sem("hT_hi_ready")
        hT_lo_ready = sem("hT_lo_ready")
        w13_hi_ready = sem("w13_hi_ready")
        w13_lo_ready = sem("w13_lo_ready")
        w2_hi_ready = sem("w2_hi_ready")
        w2_lo_ready = sem("w2_lo_ready")
        a_ready = [sem(f"a_ready{h}") for h in range(HALVES)]
        b_ready = [sem(f"b_ready{h}") for h in range(HALVES)]
        down_done = sem("down_done")
        silu_ready = [sem(f"silu_ready{h}") for h in range(HALVES)]
        gated_ready = [sem(f"gated_ready{h}") for h in range(HALVES)]
        weighed_ready = [sem(f"weighed_ready{h}") for h in range(HALVES)]
        g_hi_ready = [sem(f"g_hi_ready{h}") for h in range(HALVES)]
        g_lo_ready = [sem(f"g_lo_ready{h}") for h in range(HALVES)]
        logitT_ready = sem("logitT_ready")
        logit_ps_ready = sem("logit_ps_ready")
        logit_ready = sem("logit_ready")
        shifted_ready = sem("shifted_ready")
        expd_ready = sem("expd_ready")
        routing = sem("routing")
        route_ready = sem("route_ready")
        routeT_ps_ready = sem("routeT_ps_ready")
        routeT_ready = sem("routeT_ready")
        y_ready = sem("y_ready")
        out_ready = sem("out_ready")
        out_stored = sem("out_stored")

        x_tiled = x.rearrange("b (p j) d -> b p j d", j=JS)
        out_tiled = out.rearrange("b (p j) d -> b p (j d)", j=JS)
        cond_w_tiled = cond_w.rearrange("e (k p) o -> e p k o", p=P)

        assert BH == 2

        def slot(c):
            return 2 if c == 0 else c % 2

        def units(c):
            return M0 if c == 0 else P

        PEELED = 2
        LOOP = (PEELED, NR - 2, 2)
        assert (NSH + PEELED + 1) * P <= NSH * P + E // 2 * F and (NR - 1 - PEELED) % 2 == 0

        def condition_in(queue, engine, b):
            expert = engine.value_load(ids[0:1, b:b + 1], min_val=0, max_val=NE - 1)
            queue.dma_start(cw_raw[:, b].unsqueeze(1),
                            cond_w_tiled[bass.ds(expert, 1)].rearrange("e p k o -> p e k o")).then_inc(cw_in[b], 16)

        block = ctx.enter_context(nc.Block())

        @block.sync
        def _(sp):
            condition_in(sp, nc.sync, 0)
            sp.dma_start(x_sb[:, 2], x_tiled[2]).then_inc(x_in[2], 16)
            condition_in(sp, nc.sync, 3)
            sp.dma_start(x_sb[:, 3], x_tiled[3]).then_inc(x_in[3], 16)
            for w, src in ((0, sw1), (1, sw3)):
                sp.dma_start(w13_raw[:, KD * w:KD * w + KD, 0:M0],
                             src[:, FS - M0:FS].rearrange("(k p) f -> p k f", p=P)).then_inc(up0_in, 16)
            sp.dma_start(w13_raw[:, 0:KD, M0:M0 + E],
                         gate_w.rearrange("(k p) e -> p k e", p=P)).then_inc(up0_in, 16)
            for w, src in ((0, sw1), (1, sw3)):
                sp.dma_start(w13_raw[:, KD * w:KD * w + KD, P:NSH * P],
                             src[:, 0:FS - M0].rearrange("(k p) f -> p k f", p=P)).then_inc(up12_in, 16)
            sp.dma_start(w2_raw[0:M0, 0, :], sw2[FS - M0:FS, :]).then_inc(down0_in, 16)
            sp.dma_start(w2_raw[:, 1:NSH, :],
                         sw2[0:FS - M0, :].rearrange("(c p) d -> p c d", p=P)).then_inc(down12_in, 16)
            for g in range(2):
                for w, src in ((0, rw1), (1, rw3)):
                    for k in range(KD):
                        units_g = slice(NSH * P + g * E // 2 * F, NSH * P + (g + 1) * E // 2 * F)
                        sp.dma_start(w13_raw[:, KD * w + k, units_g].rearrange("p (e f) -> p e f", e=E // 2),
                                     src[g * E // 2:(g + 1) * E // 2, k * P:k * P + P, :]
                                     .rearrange("e p f -> p e f")).then_inc(routed_up_in[g], 16)
                if g == 0:
                    sp.dma_start(w2_raw[:, NSH:, :], rw2.rearrange("e f d -> (e f) d")
                                 .rearrange("(c p) d -> p c d", p=P)).then_inc(routed_down_in, 16)

            sp.wait_ge(routeT_ready, 1)
            sp.dma_start(dram_wT, routeT[:, :]).then_inc(routeT_out, 16)
            sp.wait_ge(routeT_out, 16)
            for r in range(NR):
                unit = r * P
                while unit < (r + 1) * P:
                    e = unit // F
                    end = min((e + 1) * F, (r + 1) * P)
                    row = dram_wT[e * NT:(e + 1) * NT, :].rearrange("t c -> (t c)").unsqueeze(0)
                    sp.dma_start(route_bc[unit - r * P:end - r * P, r, :],
                                 row.to_broadcast([end - unit, TOK])).then_inc(route_in[r >= PEELED], 16)
                    unit = end

            for b in range(B):
                sp.wait_ge(out_ready, b + 1)
                sp.dma_start(out_tiled[b], x_sb[:, b].rearrange("p j d -> p (j d)")).then_inc(out_stored, 16)
            sp.wait_ge(out_stored, 16 * B)

        def segments(chunks):
            return sum(((r + 1) * P - 1) // F - r * P // F + 1 for r in chunks)

        @block.gpsimd
        def _(pool):
            nc.gpsimd.memset(ident[:, :], 0.0).then_inc(ident_ready, 1)
            pool.dma_start(ids_bc[:, :], ids.to_broadcast([NE, B])).then_inc(ids_in, 16)
            pool.wait_ge(ident_ready, 1)
            nc.gpsimd.affine_select(out=ident[:, :], in_=ident[:, :], compare_op=ALU.not_equal, fill=1.0,
                                    base=0, pattern=[[-1, P]], channel_multiplier=1).then_inc(ident_ready, 1)
            condition_in(pool, nc.gpsimd, 2)
            nc.gpsimd.iota(expert_no[:, :], pattern=[[0, 1]], base=0, channel_multiplier=1).then_inc(expert_no_ready, 1)

            def lo_part(out_lo, raw, hi):
                return nc.gpsimd.tensor_tensor(out_lo, raw, hi.bitcast(F32), ALU.subtract)

            def cond_lo(b):
                pool.wait_ge(cw_hi_ready, b - BH + 1)
                lo_part(cw_lo[:, b - BH], cw_raw[:, b], cw_hi[:, b - BH]).then_inc(cw_lo_ready, 1)

            def w13_lo_of(c, i, first=False):
                if not first:
                    pool.wait_ge(b_ready[-1], c - 1)
                pool.wait_ge(w13_hi_ready, c + 1)
                lo_part(w13_lo[i][:, :, :], w13_raw[:, :, bass.ds(c * P, P)], w13_hi[i][:, :, :]) \
                    .then_inc(w13_lo_ready, 1)

            def w2_lo_of(c, i, first=False):
                if not first:
                    pool.wait_ge(down_done, c - 1)
                pool.wait_ge(w2_hi_ready, c + 1)
                lo_part(w2_lo[i][:, :], w2_raw[:, c, :] if isinstance(c, int) else
                        w2_raw[:, bass.ds(c, 1), :].rearrange("p c d -> p (c d)"),
                        w2_hi[i][:, :]).then_inc(w2_lo_ready, 1)

            cond_lo(2)
            cond_lo(3)
            pool.wait_ge(w13_hi_ready, 1)
            lo_part(w13_lo[0][:, 0:KD, 0:M0 + E], w13_raw[:, 0:KD, 0:M0 + E], w13_hi[0][:, 0:KD, 0:M0 + E])
            lo_part(w13_lo[0][:, KD:, 0:M0], w13_raw[:, KD:, 0:M0], w13_hi[0][:, KD:, 0:M0]) \
                .then_inc(w13_lo_ready, 1)
            w13_lo_of(1, 1, first=True)
            pool.wait_ge(w2_hi_ready, 1)
            lo_part(w2_lo[0][0:M0, :], w2_raw[0:M0, 0, :], w2_hi[0][0:M0, :]).then_inc(w2_lo_ready, 1)
            w13_lo_of(2, 0)
            w2_lo_of(1, 1, first=True)
            w13_lo_of(NSH, NSH % 2)
            w2_lo_of(2, 0)
            for c in range(NSH, NSH + PEELED):
                w2_lo_of(c, c % 2)
                w13_lo_of(c + 1, (c + 1) % 2)
            with pool.Fori(*LOOP) as r0:
                for j in range(2):
                    c = r0 + (NSH + j)
                    w2_lo_of(c, (NSH + j) % 2)
                    w13_lo_of(c + 1, (NSH + j + 1) % 2)
            w2_lo_of(NCH - 1, (NCH - 1) % 2)

        @block.scalar
        def _(act):
            nc.scalar.preload_act_table(ACT.Silu)
            act.dma_start(x_sb[:, 0], x_tiled[0]).then_inc(x_in[0], 16)
            act.dma_start(x_sb[:, 1], x_tiled[1]).then_inc(x_in[1], 16)
            act.dma_start(bias_rows[:, :], cond_b).then_inc(bias_in, 16)
            condition_in(act, nc.scalar, 1)

            def xT_hi_of(b):
                act.wait_ge(xT_ready, b + 1)
                nc.scalar.copy(xT_hi[:, b - BH, :], xT_ps[b][:, :]).then_inc(xT_hi_ready, 1)

            def cond_hi(b):
                act.wait_ge(cw_in[b], 16)
                nc.scalar.copy(cw_hi[:, b - BH], cw_raw[:, b]).then_inc(cw_hi_ready, 1)

            def hT_hi_of(b):
                for m in range(KD):
                    act.wait_ge(h_ready, KD * b + m + 1)
                    if b == 0 and m == 0:
                        act.wait_ge(biasT_ready, 1)
                    nc.scalar.activation(hT_hi[:, m, b * S:(b + 1) * S], h_ps[b][m], ACT.Identity,
                                         bias=biasT[:, m, b:b + 1]).then_inc(hT_hi_ready, 1)

            def w13_hi_of(c, i, first=False):
                if not first:
                    act.wait_ge(b_ready[-1], c - 1)
                nc.scalar.copy(w13_hi[i][:, :, :], w13_raw[:, :, bass.ds(c * P, P)]).then_inc(w13_hi_ready, 1)

            def w2_hi_of(c, i, first=False):
                if not first:
                    act.wait_ge(down_done, c - 1)
                nc.scalar.copy(w2_hi[i][:, :], w2_raw[:, c, :] if isinstance(c, int) else
                               w2_raw[:, bass.ds(c, 1), :].rearrange("p c d -> p (c d)")).then_inc(w2_hi_ready, 1)

            def silu_of(c, h, n=P, first=False):
                act.wait_ge(a_ready[h], c + 1)
                if not first:
                    act.wait_ge(gated_ready[h], c)
                nc.scalar.activation(silu_a[h][0:n, :], up_a[h][0:n, :], ACT.Silu).then_inc(silu_ready[h], 1)

            def g_hi_of(c, h, i, n=P, shared=False, reused=True):
                if shared:
                    act.wait_ge(gated_ready[h], c + 1)
                else:
                    act.wait_ge(weighed_ready[h], c + (1 - NSH))
                if reused:
                    act.wait_ge(down_done, c - 1)
                nc.scalar.copy(g_hi[i][h][0:n, :], hidden[h][0:n, :]).then_inc(g_hi_ready[h], 1)

            act.wait_ge(xT_ready, 1)
            nc.scalar.copy(xT_f32[:, 0, :], xT_ps[0][:, :]).then_inc(xT_f32_ready[0], 1)
            cond_hi(2)
            hT_hi_of(0)
            xT_hi_of(2)
            cond_hi(3)
            hT_hi_of(1)
            xT_hi_of(3)
            act.wait_ge(up0_in, 48)
            nc.scalar.copy(w13_hi[0][:, 0:KD, 0:M0 + E], w13_raw[:, 0:KD, 0:M0 + E])
            nc.scalar.copy(w13_hi[0][:, KD:, 0:M0], w13_raw[:, KD:, 0:M0]).then_inc(w13_hi_ready, 1)
            hT_hi_of(2)
            hT_hi_of(3)
            act.wait_ge(up12_in, 32)
            w13_hi_of(1, 1, first=True)
            silu_of(0, 0, n=M0, first=True)
            act.wait_ge(down0_in, 16)
            nc.scalar.copy(w2_hi[0][0:M0, :], w2_raw[0:M0, 0, :]).then_inc(w2_hi_ready, 1)
            g_hi_of(0, 0, slot(0), n=M0, shared=True, reused=False)
            silu_of(0, 1, n=M0, first=True)
            g_hi_of(0, 1, slot(0), n=M0, shared=True, reused=False)
            w13_hi_of(2, 0)
            silu_of(1, 0)
            act.wait_ge(down12_in, 16)
            w2_hi_of(1, 1, first=True)
            g_hi_of(1, 0, slot(1), shared=True, reused=False)
            silu_of(1, 1)
            act.wait_ge(shifted_ready, 1)
            nc.scalar.activation(expd[:, :, :], shifted[:, :, :], ACT.Exp).then_inc(expd_ready, 1)
            g_hi_of(1, 1, slot(1), shared=True, reused=False)
            act.wait_ge(routed_up_in[0], 16 * 2 * KD)
            w13_hi_of(3, 1)
            silu_of(2, 0)
            g_hi_of(2, 0, slot(2), shared=True, reused=False)
            act.wait_ge(routeT_ps_ready, 1)
            nc.scalar.copy(routeT[:, :], routeT_ps[0:E * NT, 0:P]).then_inc(routeT_ready, 1)
            silu_of(2, 1)
            g_hi_of(2, 1, slot(2), shared=True, reused=False)
            w2_hi_of(2, 0)

            def routed_chunk(c, i, last=False):
                w2_hi_of(c, i)
                if not last:
                    w13_hi_of(c + 1, 1 - i)
                for h in range(HALVES):
                    silu_of(c, h)
                for h in range(HALVES):
                    g_hi_of(c, h, i)

            act.wait_ge(routed_down_in, 16)
            for c in range(NSH, NSH + PEELED):
                routed_chunk(c, c % 2)
            act.wait_ge(routed_up_in[1], 16 * 2 * KD)
            with act.Fori(*LOOP) as r0:
                for j in range(2):
                    routed_chunk(r0 + (NSH + j), (NSH + j) % 2)
            routed_chunk(NCH - 1, (NCH - 1) % 2, last=True)

        @block.vector
        def _(dve):
            for e in range(E):
                last = nc.vector.memset(first_rank[:, :, e:e + 1], float(E - e))
            last.then_inc(rank_ready, 1)

            def lo_part(out_lo, value, hi):
                return nc.vector.tensor_tensor(out_lo, value, hi.bitcast(F32), ALU.subtract)

            def xT_lo_of(b):
                dve.wait_ge(xT_hi_ready, b - BH + 1)
                lo_part(xT_lo[:, b - BH, :], xT_ps[b][:, :], xT_hi[:, b - BH, :]).then_inc(xT_lo_ready, 1)

            def hT_lo_of(b):
                for m in range(KD):
                    dve.wait_ge(hT_hi_ready, KD * b + m + 1 if b < BH else KD * (b + 1))
                    cols = slice(b * S, (b + 1) * S)
                    nc.vector.scalar_tensor_tensor(
                        out=hT_lo[:, m, cols], in0=h_ps[b][m], scalar=biasT[:, m, b:b + 1],
                        in1=hT_hi[:, m, cols].bitcast(F32), op0=ALU.add, op1=ALU.subtract).then_inc(hT_lo_ready, 1)

            def gate(c, h, n=P, shared=False, first=False):
                dve.wait_ge(silu_ready[h], c + 1)
                dve.wait_ge(b_ready[h], c + 1)
                if shared and not first:
                    dve.wait_ge(g_hi_ready[h], c)
                    dve.wait_ge(g_lo_ready[h], c)
                dst = hidden[h] if shared else gated[h]
                nc.vector.tensor_tensor(dst[0:n, :], silu_a[h][0:n, :], up_b[h][0:n, :], ALU.mult) \
                    .then_inc(gated_ready[h], 1)

            def weigh(r, h):
                dve.wait_ge(gated_ready[h], r + (NSH + 1))
                dve.wait_ge(g_hi_ready[h], r + NSH)
                dve.wait_ge(g_lo_ready[h], r + NSH)
                bc = route_bc[:, bass.ds(r, 1), h * HT:(h + 1) * HT].rearrange("p r t -> p (r t)")
                nc.vector.tensor_tensor(hidden[h][:, :], gated[h][:, :], bc, ALU.mult).then_inc(weighed_ready[h], 1)

            def g_lo_of(c, h, i, n=P):
                dve.wait_ge(g_hi_ready[h], c + 1)
                lo_part(g_lo[i][h][0:n, :], hidden[h][0:n, :], g_hi[i][h][0:n, :]).then_inc(g_lo_ready[h], 1)

            def logitT_of(h):
                dve.wait_ge(a_ready[h], 1)
                nc.vector.tensor_copy(logitT[:, h * HT:(h + 1) * HT], up_a[h][M0:M0 + E, :]).then_inc(logitT_ready, 1)

            dve.wait_ge(ids_in, 16)
            dve.wait_ge(expert_no_ready, 1)
            nc.vector.tensor_scalar(one_hot[:, :], ids_bc[:, :], expert_no[:, 0:1], None, ALU.is_equal) \
                .then_inc(one_hot_ready, 1)
            dve.wait_ge(bias_ps_ready, 1)
            nc.vector.tensor_copy(biasT[:, :, :], bias_ps[:, 0:KD * B].rearrange("p (m b) -> p m b", b=B)) \
                .then_inc(biasT_ready, 1)
            dve.wait_ge(xT_ready, 2)
            nc.vector.tensor_copy(xT_f32[:, 1, :], xT_ps[1][:, :]).then_inc(xT_f32_ready[1], 1)
            dve.wait_ge(biasT_ready, 1)
            hT_lo_of(0)
            xT_lo_of(2)
            hT_lo_of(1)
            xT_lo_of(3)
            hT_lo_of(2)
            hT_lo_of(3)
            logitT_of(0)
            gate(0, 0, n=M0, shared=True, first=True)
            g_lo_of(0, 0, slot(0), n=M0)
            logitT_of(1)
            gate(0, 1, n=M0, shared=True, first=True)
            g_lo_of(0, 1, slot(0), n=M0)
            gate(1, 0, shared=True)

            chain = [0]

            def link(instruction):
                chain[0] += 1
                instruction.then_inc(routing, 1)
                dve.wait_ge(routing, chain[0])

            def over_experts(t):
                return t[:, :].unsqueeze(2).to_broadcast([P, NT, E])

            dve.wait_ge(logit_ps_ready, 1)
            link(nc.vector.tensor_copy(logit[:, :, :], logit_ps[:, 0:NT * E].rearrange("p (t e) -> p t e", e=E)))
            source = logit
            for i in range(2):
                link(nc.vector.tensor_reduce(top[i][:, :], source[:, :, :], AX.X, ALU.max))
                if i == 0:
                    nc.vector.tensor_tensor(shifted[:, :, :], logit[:, :, :], over_experts(top[0]), ALU.subtract) \
                        .then_inc(shifted_ready, 1)
                    dve.wait_ge(rank_ready, 1)
                link(nc.vector.tensor_tensor(hit[i][:, :, :], source[:, :, :], over_experts(top[i]), ALU.is_equal))
                link(nc.vector.tensor_tensor(hit_rank[i][:, :, :], hit[i][:, :, :], first_rank[:, :, :], ALU.mult))
                link(nc.vector.tensor_reduce(best_rank[i][:, :], hit_rank[i][:, :, :], AX.X, ALU.max))
                link(nc.vector.tensor_tensor(chosen[i][:, :, :], hit_rank[i][:, :, :], over_experts(best_rank[i]),
                                             ALU.is_equal))
                if i == 0:
                    link(nc.vector.scalar_tensor_tensor(out=others[:, :, :], in0=chosen[0][:, :, :], scalar=NEG_HUGE,
                                                        in1=logit[:, :, :], op0=ALU.mult, op1=ALU.add))
                    source = others
            gate(1, 1, shared=True)
            g_lo_of(1, 0, slot(1))
            link(nc.vector.tensor_tensor(both[:, :, :], chosen[0][:, :, :], chosen[1][:, :, :], ALU.add))
            dve.wait_ge(expd_ready, 1)
            nc.vector.tensor_tensor(picked[:, :, :], both[:, :, :], expd[:, :, :], ALU.mult)
            link(nc.vector.tensor_reduce(exp_sum[:, :], expd[:, :, :], AX.X, ALU.add))
            link(nc.vector.reciprocal(exp_inv[:, :], exp_sum[:, :]))
            nc.vector.tensor_tensor(route[:, :, :].rearrange("p e t -> p t e"), picked[:, :, :], over_experts(exp_inv),
                                    ALU.mult).then_inc(route_ready, 1)

            g_lo_of(1, 1, slot(1))
            for h in range(HALVES):
                gate(2, h, shared=True)
                g_lo_of(2, h, slot(2))

            def routed_chunk(r, i):
                for h in range(HALVES):
                    gate(r + NSH, h)
                    weigh(r, h)
                for h in range(HALVES):
                    g_lo_of(r + NSH, h, i)

            def add_x(b):
                dve.wait_ge(y_ready, b + 1)
                x_row = x_sb[:, b].rearrange("p j d -> p (j d)")
                nc.vector.tensor_tensor(x_row, y_acc[b][:, :], x_row, ALU.add).then_inc(out_ready, 1)

            dve.wait_ge(route_in[0], 16 * segments(range(PEELED)))
            for r in range(PEELED):
                routed_chunk(r, (NSH + r) % 2)
            dve.wait_ge(route_in[1], 16 * segments(range(PEELED, NR)))
            with dve.Fori(*LOOP) as r0:
                for j in range(2):
                    routed_chunk(r0 + j, (NSH + j) % 2)

            last = NR - 1
            for h in range(HALVES):
                gate(last + NSH, h)
                weigh(last, h)
                if h > 0:
                    add_x(0)
                g_lo_of(last + NSH, h, (NCH - 1) % 2)
            for b in range(1, B):
                add_x(b)

        @block.tensor
        def _(pe):
            def keep_warm(times):
                for _ in range(times):
                    nc.tensor.matmul(bank[2][:, 0:2 * P], nc.const_aps.tensor(1.0, [P, P], BF16),
                                     nc.const_aps.tensor(1.0, [P, 2 * P], BF16), start=True, stop=True)

            keep_warm(WARM_BEFORE_X)

            def turn_x(b):
                pe.wait_ge(x_in[b], 16)
                for k in range(KD):
                    for j in range(JS):
                        last = nc.tensor.transpose(xT_ps[b][:, k * S + j * P:k * S + (j + 1) * P],
                                                   x_sb[:, b, j, k * P:(k + 1) * P], ident[:, :])
                last.then_inc(xT_ready, 1)

            def add_products(dst, operands, start, stop):
                for n, (w, v) in enumerate(operands):
                    last = nc.tensor.matmul(dst, w, v, start=start and n == 0, stop=stop and n == len(operands) - 1)
                return last

            def three_passes(dst, quads, start, stop):
                return add_products(dst, [(w, v) for w_hi, w_lo, v_hi, v_lo in quads
                                          for w, v in ((w_hi, v_hi), (w_lo, v_hi), (w_hi, v_lo))], start, stop)

            def condition_f32(b, m):
                pe.wait_ge(xT_f32_ready[b], 1)
                pe.wait_ge(cw_in[b], 16)
                for k in range(KD):
                    last = nc.tensor.matmul(h_ps[b][m], cw_raw[:, b, k, m * P:(m + 1) * P],
                                            xT_f32[:, b, k * S:(k + 1) * S], start=(k == 0), stop=(k == KD - 1))
                last.then_inc(h_ready, 1)

            def condition_split(b):
                i = b - BH
                pe.wait_ge(xT_hi_ready, i + 1)
                pe.wait_ge(cw_hi_ready, i + 1)
                pe.wait_ge(cw_lo_ready, i + 1)
                for m in range(KD):
                    cols = slice(m * P, (m + 1) * P)
                    add_products(h_ps[b][m], [(cw[:, i, k, cols], xT_hi[:, i, k * S:(k + 1) * S])
                                              for k in range(KD) for cw in (cw_hi, cw_lo)], True, False)
                    if m == 0:
                        pe.wait_ge(xT_lo_ready, i + 1)
                    last = add_products(h_ps[b][m], [(cw_hi[:, i, k, cols], xT_lo[:, i, k * S:(k + 1) * S])
                                                     for k in range(KD)], False, True)
                last.then_inc(h_ready, KD)

            def up(c, h, i, rows=(P, P), first=False):
                pe.wait_ge(w13_hi_ready, c + 1)
                pe.wait_ge(w13_lo_ready, c + 1)
                if not first:
                    pe.wait_ge(gated_ready[h], c)
                toks = slice(h * HT, (h + 1) * HT)
                for w, (dst, ready) in enumerate(((up_a[h], a_ready[h]), (up_b[h], b_ready[h]))):
                    n = rows[w]
                    last = three_passes(dst[0:n, :],
                                        [(w13_hi[i][:, KD * w + k, 0:n], w13_lo[i][:, KD * w + k, 0:n],
                                          hT_hi[:, k, toks], hT_lo[:, k, toks]) for k in range(KD)], True, True)
                    last.then_inc(ready, 1)

            def down(c, h, wi, gi, n=P, start=False, stop=False):
                pe.wait_ge(w2_hi_ready, c + 1)
                pe.wait_ge(w2_lo_ready, c + 1)
                pe.wait_ge(g_hi_ready[h], c + 1)
                pe.wait_ge(g_lo_ready[h], c + 1)
                for b in range(BH):
                    for j in range(JS):
                        toks = slice(b * S + j * P, b * S + (j + 1) * P)
                        last = three_passes(y_acc[h * BH + b][:, j * D:(j + 1) * D],
                                            [(g_hi[gi][h][0:n, toks], g_lo[gi][h][0:n, toks],
                                              w2_hi[wi][0:n, :], w2_lo[wi][0:n, :])],
                                            start and j == 0, stop and j == JS - 1)
                    if stop:
                        last.then_inc(y_ready, 1)
                if not stop and h == HALVES - 1:
                    last.then_inc(down_done, 1)

            pe.wait_ge(ident_ready, 2)
            turn_x(0)
            keep_warm(WARM_BEFORE_CONDITION)
            turn_x(1)
            pe.wait_ge(one_hot_ready, 1)
            pe.wait_ge(bias_in, 16)
            for m in range(KD):
                last = nc.tensor.matmul(bias_ps[:, m * B:(m + 1) * B], bias_rows[:, m * P:(m + 1) * P], one_hot[:, :],
                                        start=True, stop=True)
            last.then_inc(bias_ps_ready, 1)
            condition_f32(0, 0)
            condition_f32(0, 1)
            turn_x(2)
            condition_f32(1, 0)
            condition_f32(1, 1)
            pe.wait_ge(biasT_ready, 1)
            turn_x(3)
            condition_split(2)
            condition_split(3)
            pe.wait_ge(hT_hi_ready, KD * BH)
            pe.wait_ge(hT_lo_ready, KD * BH)
            up(0, 0, 0, rows=(M0 + E, M0), first=True)
            pe.wait_ge(hT_hi_ready, KD * B)
            pe.wait_ge(hT_lo_ready, KD * B)
            up(0, 1, 0, rows=(M0 + E, M0), first=True)
            up(1, 0, 1)
            pe.wait_ge(logitT_ready, HALVES)
            for t in range(NT):
                last = nc.tensor.transpose(logit_ps[:, t * E:(t + 1) * E], logitT[:, t * P:(t + 1) * P],
                                           ident[0:E, 0:E])
            last.then_inc(logit_ps_ready, 1)
            up(1, 1, 1)
            up(2, 0, 0)
            down(0, 0, 0, slot(0), n=M0, start=True)
            pe.wait_ge(route_ready, 1)
            nc.tensor.transpose(routeT_ps[0:E * NT, 0:P], route[:, :, :].rearrange("p e t -> p (e t)"), ident[:, :]) \
                .then_inc(routeT_ps_ready, 1)
            up(2, 1, 0)
            pe.wait_ge(routeT_ready, 1)
            down(0, 1, 0, slot(0), n=M0, start=True)
            for h in range(HALVES):
                down(1, h, 1, slot(1))

            def routed_chunk(c, i):
                for h in range(HALVES):
                    up(c, h, i)
                for h in range(HALVES):
                    down(c - 1, h, 1 - i, 1 - i)

            for c in range(NSH, NSH + PEELED):
                routed_chunk(c, c % 2)
            with pe.Fori(*LOOP) as r0:
                for j in range(2):
                    routed_chunk(r0 + (NSH + j), (NSH + j) % 2)
            i = (NCH - 1) % 2
            for h in range(HALVES):
                up(NCH - 1, h, i)
            down(NCH - 2, 0, 1 - i, 1 - i)
            down(NCH - 1, 0, i, i, stop=True)
            down(NCH - 2, 1, 1 - i, 1 - i)
            down(NCH - 1, 1, i, i, stop=True)


_INS = ['x', 'itok_B_0_15', 'L0_cond_W', 'L0_cond_b', 'L0_ffn_gate_w', 'L0_ffn_sw1', 'L0_ffn_sw2', 'L0_ffn_sw3',
        'L0_ffn_rw1', 'L0_ffn_rw2', 'L0_ffn_rw3']


def kernel(**inputs):
    import numpy as _np
    import concourse.bacc as _bacc
    from concourse import mybir as _mybir
    from concourse.bass_utils import run_bass_kernel_spmd as _run

    nc = _bacc.Bacc("TRN2", target_bir_lowering=False, num_devices=1)
    arrays, args = {}, []
    for name in _INS:
        a = _np.ascontiguousarray(inputs[name])
        if name == 'itok_B_0_15':
            a = a.reshape(1, -1)
        arrays[f"in_{name}_dram"] = a
        args.append(nc.dram_tensor(f"in_{name}_dram", a.shape, _mybir.dt.from_np(a.dtype), kind="ExternalInput").ap())
    x = arrays["in_x_dram"]
    out = nc.dram_tensor("out_dram", x.shape, _mybir.dt.from_np(x.dtype), kind="ExternalOutput").ap()
    adaln_moe_ffn(nc, *args, out)
    r = _run(nc, [arrays], core_ids=[0])
    return r.results[0]["out_dram"]
```
